# Optimizing a Trainium2 kernel written in Bass

```python
import numpy as np
import jax
import jax.numpy as jnp

def _softmax(x, axis=-1):
    return jax.nn.softmax(x, axis=axis)

def _gelu(x):
    return jax.nn.gelu(x, approximate=True)

def _silu(x):
    return jax.nn.silu(x)

def _sigmoid(x):
    return jax.nn.sigmoid(x)

def _layernorm(x, axis=-1, eps=1e-05):
    m = jnp.mean(x, axis=axis, keepdims=True)
    v = jnp.var(x, axis=axis, keepdims=True)
    return (x - m) / jnp.sqrt(v + eps)

def _scatter_add(tgt, idx, src, axis=0):
    return tgt.at[idx].add(src)

def _segment_sum(src, seg, n):
    return jax.ops.segment_sum(src, seg, n)
kernel_name = 'mk_adj_preln_d2_adj_r2_67c38e'

def setup_inputs(seed: int=0):
    np.random.seed(seed)
    _w = jnp.asarray

    def _rec_inputs():
        import jax
        import jax.numpy as jnp
        _gk = jax.random.key(seed)
        x = -0.006082 + 1.001 * jax.random.normal(jax.random.fold_in(_gk, 1), (8192, 64), jnp.float32)
        _w = (1.0 + jnp.arange(8192, dtype=jnp.float32)) ** (-0.5)
        _w = _w / _w.mean()
        _pij = jnp.clip(0.000244141 * _w[:, None] * _w[None, :], 0.0, 1.0)
        _a = jax.random.uniform(jax.random.fold_in(_gk, 2), (8192, 8192)) < _pij
        adj = _a.astype(jnp.int32)
        return (x, adj)
    x, adj = _rec_inputs()

    def _L0_gnn_setup():
        import jax, jax.numpy as jnp
        import numpy as np
        ALPHA = 0.2
        NEG_INF = -9000000000000000.0
        key = jax.random.key(seed)
        k1, k2, k3, k4 = jax.random.split(key, 4)
        N, F_IN, F_OUT = (512, 64, 64)
        h = jax.random.normal(k1, (N, F_IN), dtype=jnp.float32)
        adj = jax.random.randint(k2, (N, N), 0, 2, dtype=jnp.int32)
        lim_W = 1.414 * np.sqrt(6.0 / (F_IN + F_OUT))
        W = jax.random.uniform(k3, (F_IN, F_OUT), minval=-lim_W, maxval=lim_W, dtype=jnp.float32)
        lim_a = 1.414 * np.sqrt(6.0 / (2 * F_OUT + 1))
        a = jax.random.uniform(k4, (2 * F_OUT, 1), minval=-lim_a, maxval=lim_a, dtype=jnp.float32)
        return {'h': h, 'adj': adj, 'W': W, 'a': a}
    _L0_gnn_all = _L0_gnn_setup()
    _L0_gnn_in = {k: v for k, v in _L0_gnn_all.items() if k in ('W', 'a')}
    del _L0_gnn_all

    def _L1_gnn_setup():
        import jax, jax.numpy as jnp
        import numpy as np
        ALPHA = 0.2
        MASK_VAL = -9000000000000000.0
        key = jax.random.key(seed)
        k1, k2, k3 = jax.random.split(key, 3)
        N, D = (4096, 64)
        h = jax.random.normal(k1, (N, D), dtype=jnp.float32)
        adj = jax.random.randint(k2, (N, N), 0, 2, dtype=jnp.int32)
        a = jax.random.normal(k3, (2 * D, 1), dtype=jnp.float32) * (1.414 / np.sqrt(D))
        return {'h': h, 'adj': adj, 'a': a}
    _L1_gnn_all = _L1_gnn_setup()
    _L1_gnn_in = {k: v for k, v in _L1_gnn_all.items() if k in ('a',)}
    del _L1_gnn_all
    return {'x': x, 'adj': adj, 'L0_gnn_W': _L0_gnn_in['W'], 'L0_gnn_a': _L0_gnn_in['a'], 'L1_gnn_a': _L1_gnn_in['a']}

def reference(x, adj, L0_gnn_W, L0_gnn_a, L1_gnn_a):
    import jax
    import jax.numpy as jnp

    def _L0_gnn_ref(h, adj, W, a):
        import jax, jax.numpy as jnp
        import numpy as np
        ALPHA = 0.2
        NEG_INF = -9000000000000000.0
        F_OUT = W.shape[1]
        Wh = h @ W
        a1, a2 = (a[:F_OUT, 0], a[F_OUT:, 0])
        e = (Wh @ a1)[:, None] + (Wh @ a2)[None, :]
        e = jax.nn.leaky_relu(e, negative_slope=ALPHA)
        scores = jnp.where(adj > 0, e, jnp.float32(NEG_INF))
        attention = jax.nn.softmax(scores, axis=1)
        h_prime = attention @ Wh
        return jax.nn.elu(h_prime)

    def _L1_gnn_ref(h, adj, a):
        import jax, jax.numpy as jnp
        import numpy as np
        ALPHA = 0.2
        MASK_VAL = -9000000000000000.0
        D = h.shape[1]
        wh1 = h @ a[:D, :]
        wh2 = h @ a[D:, :]
        e = wh1 + wh2.T
        e = jnp.where(e > 0, e, ALPHA * e)
        scores = jnp.where(adj > 0, e, MASK_VAL)
        attention = jax.nn.softmax(scores, axis=1)
        h_prime = attention @ h
        return jax.nn.relu(h_prime)
    h = jnp.maximum(_layernorm(x, axis=-1), 0.0)
    x = x + _L0_gnn_ref(h, adj, L0_gnn_W, L0_gnn_a)
    h = jnp.maximum(_layernorm(x, axis=-1), 0.0)
    x = x + _L1_gnn_ref(h, adj, L1_gnn_a)
    return x

_drawn_inputs = setup_inputs


def setup_inputs(seed=0):
    import zlib

    import numpy as np

    out = dict(_drawn_inputs(seed))
    spreads = {}
    factors = {}
    for name, (base, spread) in spreads.items():
        noise = np.random.default_rng([zlib.crc32(name.encode()), seed]).standard_normal(out[name].shape)
        drawn = base * np.exp(spread * noise) if base else spread * noise
        out[name] = jnp.asarray(drawn.astype(out[name].dtype))
    for name, factor in factors.items():
        out[name] = (out[name] * factor).astype(out[name].dtype)
    return out
```

```python
import concourse.bass as bass
from concourse import mybir
from contextlib import ExitStack

F32 = mybir.dt.float32
F16 = mybir.dt.float16
I32 = mybir.dt.int32
U32 = mybir.dt.uint32
I16 = mybir.dt.int16
ALU = mybir.AluOpType
ACT = mybir.ActivationFunctionType
AX = mybir.AxisListType

P = 128
ALPHA = 0.2
EPS = 1e-5
MASKED = -9.0e15
FLOOR = -1.0e15
BITS = 16
EXPONENT = 0x7F800000
SEG = 8

HEAD = {0: [(2, 16), (2, 4), (4, 2), (8, 1)], 1: [(3, 8)]}
CLASSES = [(2, 6, [(3, 8)]), (6, 30, [(2, 4)]), (30, 64, [(2, 2)])]


def units_of(t):
    if t in HEAD:
        return HEAD[t]
    return next(units for a, b, units in CLASSES if a <= t < b)


def chunks_of(t):
    return sum(c for _, c in units_of(t))


def segments_of(units):
    out, at = [], 0
    for u, (_, c) in enumerate(units):
        for k in range(0, c, SEG):
            out.append((u, at + k, k * P, min(SEG, c - k)))
        at += c
    return out


def groups_of(t):
    return -(-chunks_of(t) // 4)


def extract_steps(t):
    rounds, units = sum(r for r, _ in units_of(t)), len(units_of(t))
    return 8 * rounds - 1 + 2 * units + 6 + (units > 1) + 2 * (t > 0)


def score_steps(t):
    segments = len(segments_of(units_of(t)))
    return segments + (segments > 1)


class Tile:

    def __init__(self, t, i=0):
        def so_far(of, tiles=None, per_turn=2):
            return sum(of(k) for k in (range(t) if tiles is None else tiles)) + i * (per_turn * of(t))

        self.t, self.par, self.turn = t + 2 * i, t % 2, t // 2 + i
        self.units, self.static = units_of(t), t
        self.chunks = chunks_of(t)
        self.segments = segments_of(self.units)
        self.groups = groups_of(t)
        self.slots = 8 * sum(r for r, _ in self.units)
        self.chunk = so_far(chunks_of)
        self.unit = so_far(lambda k: len(units_of(k)))
        self.segment = so_far(lambda k: len(segments_of(units_of(k))))
        self.group = so_far(groups_of)
        self.group0 = sum(groups_of(k) for k in range(t))
        self.chunks_here = so_far(chunks_of, range(t % 2, t, 2), 1)
        self.extract_step = so_far(extract_steps)
        self.score_step = so_far(score_steps)


def each_tile(eng, tiles, step):
    t = 0
    while t < tiles:
        loop = next((b for a, b, _ in CLASSES if a + 2 == t and b - t >= 4), None)
        if loop is None:
            step(Tile(t), Tile(t - 1) if t else None)
            t += 1
        else:
            with eng.Fori(0, (loop - t) // 2) as i:
                step(Tile(t, i), Tile(t - 1, i))
                step(Tile(t + 1, i), Tile(t, i))
            t = loop
    step(None, Tile(tiles - 1))


def gat_kernel(nc, x_d, adj_d, w_d, a0_d, a1_d, out_d):
    N, D = x_d.shape
    NT = N // P
    WORDS = N // BITS
    HALF = N // 2
    NCH = sum(chunks_of(t) for t in range(NT))
    NU = sum(len(units_of(t)) for t in range(NT))
    C0 = chunks_of(0)
    KMAX = max(8 * r for t in range(NT) for r, _ in units_of(t))
    EMAX = P * max(c for t in range(NT) for _, c in units_of(t))
    SLOTS = 8 * sum(r for r, _ in units_of(0))
    R = D + 2
    RG = D + 1
    SHIFT = KMAX

    table_d = [nc.dram_tensor(f"table{n}", (N, RG), F32, kind="Internal").ap() for n in range(2)]
    s2_d = [nc.dram_tensor(f"s2_{n}", (NT, P), F32, kind="Internal").ap() for n in range(2)]
    x1_d = nc.dram_tensor("x1_scratch", (P, NT * D), F32, kind="Internal").ap()

    ctx = ExitStack()
    with ctx:
        def sb(name, shape, dt):
            return ctx.enter_context(nc.sbuf_tensor(name, shape, dt))

        def sem(name):
            return ctx.enter_context(nc.semaphore(name))

        adj = [sb(f"adj{b}", [P, N], I32) for b in range(2)]
        signs = [sb(f"signs{b}", [P, HALF], F16) for b in range(2)]
        table = sb("table", [P, NT * R], F32)
        table3 = table[:, :].rearrange("p (t r) -> p t r", r=R)
        agg = sb("agg", [P, NT * D], F32)
        agg3 = agg[:, :].rearrange("p (t d) -> p t d", d=D)

        identity = sb("identity", [P, P], F32)
        ident16 = sb("ident16", [P, P], F16)
        weights = sb("weights", [P, BITS * P], F16)
        quarter = sb("quarter", [P, P], F16)
        ones16 = sb("ones16", [P, 512], F16)
        before = sb("before", [P, P], F16)
        mean_of = sb("mean_of", [P, P], F32)
        word_no = sb("word_no", [P, WORDS], I32)
        edge_no = sb("edge_no", [P, SHIFT + EMAX], I16)
        select = sb("select", [SEG, SEG * P], F32)

        keys = sb("keys", [P, WORDS], F32)
        kept = sb("kept", [P, WORDS], F32)
        taken = sb("taken", [P, WORDS], F32)
        words = sb("words", [P, WORDS], F32)
        found = sb("found", [P, SLOTS], F32)
        ranked = sb("ranked", [P, SLOTS], F32)
        exponent = sb("exponent", [P, SLOTS], I32)
        word_of = sb("word_of", [P, SLOTS], I32)
        bit1 = sb("bit1", [P, SLOTS], F32)
        valid = sb("valid", [P, SLOTS], F32)
        values = [sb(f"values{b}", [P, 2 * SLOTS], F16) for b in range(2)]
        count = sb("count", [P, 4], F32)
        count16 = [sb(f"count16_{b}", [P, 4], F16) for b in range(2)]
        degree = [sb(f"degree{b}", [P, 2], F32) for b in range(2)]
        place = sb("place", [P, KMAX + EMAX], F16)
        first = sb("first", [P, 4], F32)
        start_m = sb("start_m", [P, 4], F32)
        edge_f = sb("edge_f", [P, C0], F32)
        missed = sb("missed", [P, NT], F32)
        beyond = sb("beyond", [P, NU], F32)
        middle = sb("middle", [P, NU], F32)
        reach = sb("reach", [P, NU], F32)
        index_all = sb("index_all", [P, NCH], U32)
        fault = sb("fault", [P, 4], F32)
        flag = sb("flag", [1, 1], I32)

        index = [sb(f"index{b}", [P, C0 if b == 0 else SEG], U32) for b in range(2)]
        rows = [sb("rows0", [P, C0 * RG], F32), sb("rows1", [P, SEG * RG], F32)]
        s2T = sb("s2T", [SEG, P], F32)
        slope = sb("slope", [P, SEG * P], F32)
        mask = sb("mask", [P, SEG * P], F32)
        leaky = sb("leaky", [P, SEG * P], F32)
        small_scores = [sb(f"scores{b}", [P, SEG * P], F32) for b in range(2)]
        big_scores = agg[:, NT * D - C0 * P:NT * D]
        top = sb("top", [P, 8], F32)
        shift = [sb(f"shift{b}", [P, 1], F32) for b in range(2)]
        den = [sb(f"den{b}", [P, 1], F32) for b in range(2)]
        den_all = sb("den_all", [P, NT], F32)
        s1s = sb("s1s", [P, NT], F32)
        probsT = [sb(f"probsT{b}", [P, 512], F32) for b in range(2)]
        mean_row = sb("mean_row", [P, D], F32)
        stat = sb("stat", [P, 5 * NT], F32)
        w_sb = sb("w_sb", [D, R], F32)
        wT = sb("wT", [D, D], F32)
        a_sb = sb("a_sb", [D, 4], F32)
        hT = [sb(f"hT{b}", [D, 4 * P], F32) for b in range(2)]

        SZ = NT * D
        bufs = [adj[b][:, k * SZ:(k + 1) * SZ].bitcast(F32) for b in range(2) for k in range(2)]
        x_b, exp_b, centred_b, square_b = bufs
        s2_row = adj[1][:, :].bitcast(F32)
        dense_scores = adj[0][:, :].bitcast(F32)

        def by_tile(ap, width=D):
            return ap.rearrange("p (t d) -> p t d", d=width)

        def ps(name, shape, dt=F32):
            return ctx.enter_context(nc.psum_tensor(name, shape, dt))

        packed = [ps(f"packed{b}", [P, WORDS]) for b in range(2)]
        edges_ps = ps("edges_ps", [P, 512])
        s2T_ps = ps("s2T_ps", [P, 512])
        s2_ps = ps("s2_ps", [P, SEG * P])
        turned_ps = ps("turned_ps", [P, 512])
        sum_ps = ps("sum_ps", [P, 512])
        hT_ps = [turned_ps, s2T_ps]
        starts_ps = s2T_ps
        rows_ps = [s2_ps[:, 0:512], s2_ps[:, 512:1024]]

        consts = sem("consts_made")
        x_in, w_in = sem("x_in"), sem("w_in")
        adj_in = [sem(f"adj_in{b}") for b in range(2)]
        casts, packs, counted = sem("signs_made"), sem("halves_packed"), sem("edges_counted")
        based, placed, edged = sem("first_edges_summed"), sem("places_made"), sem("edges_packed")
        indexed = sem("indices_made")
        dve_x, dve_c = sem("dve_extract_step"), sem("dve_const_step")
        gates = sem("gate")
        fault_made, fault_sum, flag_made = sem("fault_made"), sem("fault_summed"), sem("flag_made")
        dve_f = sem("dve_fault_step")

        class Layer:
            def __init__(self, n):
                def s(name):
                    return sem(f"{name}_{n}")
                self.n = n
                self.h_made, self.wT_ps, self.wT_made, self.wa_ps, self.wa_made = (
                    s("h_made"), s("wT_ps"), s("wT_made"), s("wa_ps"), s("wa_made"))
                self.hT_ps, self.hT_made, self.rows_ps, self.rows_made = (
                    s("hT_ps"), s("hT_made"), s("rows_ps"), s("rows_made"))
                self.mean_ps, self.mean_made, self.stored = s("mean_ps"), s("mean_made"), s("table_stored")
                self.index_copied = s("index_copied")
                self.rows_in = [s(f"rows_in{b}") for b in range(2)]
                self.s2T_turned, self.s2T_made, self.s2_spread = s("s2T_turned"), s("s2T_made"), s("s2_spread")
                self.masked, self.distance_made = s("masked"), s("distance_made")
                self.slope_made, self.s2_read, self.dve = s("slope_made"), s("s2_read"), s("dve_score_step")
                self.shifted, self.probs_made = s("shifted"), s("probs_made")
                self.turned, self.turned_copied, self.group_summed = s("turned"), s("turned_copied"), s("group_summed")
                self.finished = s("tile_finished")
                self.d_s2, self.d_in, self.d_dve = s("dense_s2"), s("dense_adj_in"), s("dense_dve_step")
                self.d_shift, self.d_probs, self.d_turned = s("dense_shifted"), s("dense_probs"), s("dense_turned")
                self.d_copied, self.d_summed, self.d_done = s("dense_copied"), s("dense_summed"), s("dense_tile_done")
                self.post, self.var_made, self.root_made = s("dve_post_step"), s("var_made"), s("root_made")
                self.neg_made, self.exp_made = s("neg_made"), s("exp_made")
                self.x_in, self.x_out = s("x_again"), s("x_stored")

        layers = [Layer(0), Layer(1)]

        block = ctx.enter_context(nc.Block())

        class Steps:

            def __init__(self, eng, s, base=0):
                self.eng, self.s, self.base, self.n = eng, s, base, 0

            def inc(self, ins):
                self.n += 1
                ins.then_inc(self.s, 1)

            def wait(self):
                self.eng.wait_ge(self.s, self.base + self.n)

            def __call__(self, ins):
                self.inc(ins)
                self.wait()

        def gate(eng):
            eng.sem_inc(gates, 1)

        x_v = x_d.rearrange("(t p) d -> p t d", p=P)
        out_v = out_d.rearrange("(t p) d -> p t d", p=P)
        adj_v = adj_d.rearrange("(t p) n -> t p n", p=P)
        table_v = [table_d[n].rearrange("(t p) r -> p t r", p=P) for n in range(2)]

        def col(ap, at, n=1):
            return ap[:, bass.ds(at, n)]

        def groups_before(cur):
            return cur.group - groups_of(cur.static - 1)

        def scores_of(tile):
            if tile.static == 0:
                return big_scores
            return small_scores[tile.par][:, 0:tile.chunks * P]

        @block.sync
        def _(sp):
            def load_x():
                sp.dma_start(by_tile(agg[:, :]), x_v).then_inc(x_in, 16)

            def load_weights():
                sp.dma_start(w_sb[:, 0:D], w_d).then_inc(w_in, 16)
                for n, a_d in enumerate((a0_d, a1_d)):
                    sp.dma_start(a_sb[:, 2 * n:2 * n + 1], a_d[D:2 * D, :]).then_inc(w_in, 16)
                    sp.dma_start(a_sb[:, 2 * n + 1:2 * n + 2], a_d[0:D, :]).then_inc(w_in, 16)

            def load_adjacency():
                for b in range(2):
                    sp.dma_start(adj[b][:, :], adj_v[b]).then_inc(adj_in[b], 16)
                with sp.Fori(0, NT // 2 - 1) as i:
                    for b in range(2):
                        sp.wait_ge(casts, i * 4 + 2 * b + 2)
                        sp.dma_start(adj[b][:, :], adj_v[i * 2 + (2 + b)]).then_inc(adj_in[b], 16)

            def store_table(L):
                sp.wait_ge(L.rows_made, NT // 4)
                if L.n == 1:
                    sp.wait_ge(L.h_made, 1)
                sp.dma_start(table_v[L.n], table3[:, :, 0:RG]).then_inc(L.stored, 16)
                sp.wait_ge(L.stored, 16)

            def dense_loads(L):
                with nc.allow_non_contiguous_dma(reason="one column, on the dense path alone"):
                    sp.dma_start(s2_d[L.n].rearrange("t p -> p t"), table3[:, :, D]).then_inc(L.d_s2, 16)
                sp.wait_ge(L.d_s2, 16)
                sp.dma_start(s2_row, s2_d[L.n].rearrange("t p -> (t p)")[None, :].to_broadcast((P, N))
                             ).then_inc(L.d_s2, 16)
                with sp.Fori(0, NT) as i:
                    sp.wait_ge(L.d_done, i)
                    sp.dma_start(adj[0][:, :], adj_v[i]).then_inc(L.d_in, 16)

            load_x()
            load_weights()
            load_adjacency()
            store_table(layers[0])
            sp.wait_ge(flag_made, 1)
            dense = sp.value_load(flag[0:1, 0:1], min_val=0, max_val=1)
            with sp.If(dense > 0):
                dense_loads(layers[0])
            sp.wait_ge(layers[0].post, 1)
            sp.dma_start(by_tile(x_b), x_v).then_inc(layers[0].x_in, 16)
            sp.wait_ge(layers[0].x_out, 1)
            sp.dma_start(x1_d, agg[:, :]).then_inc(layers[0].x_in, 16)
            sp.wait_ge(layers[0].x_in, 32)
            store_table(layers[1])
            with sp.If(dense > 0):
                dense_loads(layers[1])
            sp.wait_ge(layers[1].post, 1)
            sp.dma_start(x_b, x1_d).then_inc(layers[1].x_in, 16)
            sp.wait_ge(layers[1].x_out, 1)
            sp.dma_start(out_v, by_tile(agg[:, :])).then_inc(layers[1].x_in, 16)
            sp.wait_ge(layers[1].x_in, 32)

        @block.gpsimd
        def _(pool):
            nc.gpsimd.iota(word_no[:, :], [[1, WORDS]], base=0, channel_multiplier=0).then_inc(consts, 1)
            nc.gpsimd.iota(edge_no[:, :], [[1, SHIFT + EMAX]], base=-SHIFT, channel_multiplier=0,
                           allow_small_or_imprecise_dtypes=True).then_inc(consts, 1)

            nc.gpsimd.memset(identity[:, :], 0.0).then_inc(consts, 1)
            nc.gpsimd.memset(before[:, :], 1.0).then_inc(consts, 1)
            pool.wait_ge(consts, 4)
            nc.gpsimd.affine_select(out=identity[:, :], in_=identity[:, :], compare_op=ALU.not_equal,
                                    fill=1.0, base=0, pattern=[[-1, P]], channel_multiplier=1
                                    ).then_inc(consts, 1)
            nc.gpsimd.affine_select(out=before[:, :], in_=before[:, :], compare_op=ALU.is_gt,
                                    fill=0.0, base=0, pattern=[[1, P]], channel_multiplier=-1
                                    ).then_inc(consts, 1)

            def gathers(L):
                pool.wait_ge(L.stored, 16)
                pool.wait_ge(indexed, NT)

                def step(cur, prev):
                    if cur is None:
                        return
                    if cur.static >= 2:
                        pool.wait_ge(L.group_summed, groups_before(cur))
                    nc.gpsimd.tensor_copy(index[cur.par][:, 0:cur.chunks],
                                          col(index_all, cur.chunk, cur.chunks)).then_inc(L.index_copied, 1)
                    pool.wait_ge(L.index_copied, cur.t + 1)
                    gate(pool)
                    for c in range(cur.chunks):
                        nc.gpsimd.indirect_dma_start(
                            rows[cur.par][:, c * RG:(c + 1) * RG], None, table_d[L.n],
                            bass.IndirectOffsetOnAxis(ap=index[cur.par][:, c:c + 1], axis=0)
                        ).then_inc(L.rows_in[cur.par], 16)

                each_tile(pool, NT, step)

            pool.wait_ge(flag_made, 1)
            dense = pool.value_load(flag[0:1, 0:1], min_val=0, max_val=1)
            for L in layers:
                with pool.If(dense < 1):
                    gathers(L)

        @block.scalar
        def _(act):
            def make_table(L):
                if L.n == 0:
                    act.wait_ge(L.wT_ps, 1)
                    nc.scalar.copy(wT[:, :], sum_ps[0:D, 0:D]).then_inc(L.wT_made, 1)
                    act.wait_ge(L.wa_ps, 1)
                    nc.scalar.copy(w_sb[:, D:R], sum_ps[0:D, 64:66]).then_inc(L.wa_made, 1)
                for q in range(NT // 4):
                    act.wait_ge(L.hT_ps, q + 1)
                    if q >= 2:
                        act.wait_ge(L.rows_ps, q - 1)
                    nc.scalar.copy(hT[q % 2][:, :], hT_ps[q % 2][0:D, :]).then_inc(L.hT_made, 1)

            def root(L):
                act.wait_ge(L.var_made, 1)
                nc.scalar.activation(stat[:, NT:2 * NT], stat[:, 0:NT], ACT.Sqrt).then_inc(L.root_made, 1)

            def cast():
                def step(cur, prev):
                    if cur is None:
                        return
                    act.wait_ge(adj_in[cur.par], cur.turn * 16 + 16)
                    for h in range(2):
                        if cur.static >= 1:
                            act.wait_ge(packs, cur.t * 2 - 1 + h)
                        if cur.static >= 2 and h == 0:
                            act.wait_ge(counted, cur.t - 1)
                        gate(act)
                        nc.scalar.activation(signs[h][:, :], adj[cur.par][:, h * HALF:(h + 1) * HALF],
                                             ACT.Sign, accum_out=degree[cur.par][:, h:h + 1]
                                             ).then_inc(casts, 1)

                each_tile(act, NT, step)

            def attend(L):
                def front(cur):
                    for k, (u, c0, e0, nc_) in enumerate(cur.segments):
                        g = cur.segment + k
                        act.wait_ge(L.s2T_turned, g + 1)
                        nc.scalar.copy(s2T[0:nc_, :], s2T_ps[0:nc_, 0:P]).then_inc(L.s2T_made, 1)
                        act.wait_ge(L.s2_spread, g + 1)
                        if cur.static or k:
                            act.wait_ge(L.s2_read, g)
                        gate(act)
                        nc.scalar.activation(slope[:, 0:nc_ * P], s2_ps[:, 0:nc_ * P], ACT.Identity,
                                             bias=col(s1s, cur.t), scale=ALPHA).then_inc(L.slope_made, 1)
                        if cur.static or k:
                            act.wait_ge(L.masked, g)
                        gate(act)
                        nc.scalar.activation(mask[:, 0:nc_ * P], edge_no[:, SHIFT + e0:SHIFT + e0 + nc_ * P],
                                             ACT.Abs, bias=col(middle, cur.unit + u)
                                             ).then_inc(L.distance_made, 1)

                def back(prev):
                    act.wait_ge(L.shifted, prev.t + 1)
                    gate(act)
                    sc = scores_of(prev)
                    nc.scalar.activation(sc, sc, ACT.Exp, bias=shift[prev.par][:, :],
                                         accum_out=den[prev.par][:, :]).then_inc(L.probs_made, 1)
                    for k in range(prev.groups):
                        n = min(4, prev.chunks - 4 * k) * P
                        act.wait_ge(L.turned, prev.group + (k + 1))
                        if prev.group0 + k >= 2:
                            act.wait_ge(L.group_summed, prev.group + k - 1)
                        gate(act)
                        nc.scalar.copy(probsT[(prev.group0 + k) % 2][:, 0:n], turned_ps[:, 0:n]
                                       ).then_inc(L.turned_copied, 1)

                def step(cur, prev):
                    if cur:
                        front(cur)
                    if prev:
                        back(prev)

                each_tile(act, NT, step)

            def dense_attend(L):
                with act.Fori(0, NT) as i:
                    act.wait_ge(L.d_shift, i + 1)
                    gate(act)
                    nc.scalar.activation(dense_scores, dense_scores, ACT.Exp, bias=shift[0][:, :],
                                         accum_out=den[0][:, :]).then_inc(L.d_probs, 1)

            root(layers[0])
            make_table(layers[0])
            cast()
            act.wait_ge(flag_made, 1)
            dense = act.value_load(flag[0:1, 0:1], min_val=0, max_val=1)
            for L in layers:
                with act.If(dense > 0) as other:
                    dense_attend(L)
                with act.If(dense < 1):
                    attend(L)
                if L.n == 0:
                    act.wait_ge(L.neg_made, 1)
                    nc.scalar.activation(exp_b, exp_b, ACT.Exp).then_inc(L.exp_made, 1)
                    root(layers[1])
                    make_table(layers[1])

        @block.vector
        def _(dve):
            V = nc.vector

            def make_consts():
                c = Steps(dve, dve_c)
                dve.wait_ge(consts, 6)
                c.inc(V.tensor_copy(ident16[:, :], identity[:, :]))
                c.inc(V.memset(ones16[:, :], 1.0))
                c.inc(V.memset(mean_of[:, :], 1.0 / N))
                c.inc(V.tensor_copy(select[:, :].rearrange("k (c p) -> k c p", p=P),
                                    identity[0:SEG, 0:SEG].unsqueeze(2).to_broadcast((SEG, SEG, P))))
                c.inc(V.tensor_scalar(quarter[:, :], identity[:, :], 0.25, None, ALU.mult))
                for b in range(BITS):
                    c.inc(V.tensor_scalar(weights[:, b * P:(b + 1) * P], identity[:, :], float(1 << b),
                                          None, ALU.mult))
                c.wait()

            def normalise(L, c, src, centred, square, out):
                mean, var = stat[:, 4 * NT:5 * NT], stat[:, 0:NT]
                c(V.tensor_reduce(mean, by_tile(src), AX.X, ALU.add))
                c(V.tensor_scalar(mean, mean, 1.0 / D, None, ALU.mult))
                c(V.tensor_tensor(by_tile(centred), by_tile(src),
                                  mean.unsqueeze(2).to_broadcast((P, NT, D)), ALU.subtract))
                c(V.tensor_tensor(square, centred, centred, ALU.mult))
                c(V.tensor_reduce(var, by_tile(square), AX.X, ALU.add))
                c(V.tensor_scalar(var, var, 1.0 / D, EPS, ALU.mult, ALU.add))
                V.tensor_copy(mean, var).then_inc(L.var_made, 1)
                dve.wait_ge(L.root_made, 1)
                y, z = stat[:, 2 * NT:3 * NT], stat[:, 3 * NT:4 * NT]
                c(V.reciprocal(y, stat[:, NT:2 * NT]))
                c(V.tensor_tensor(z, y, y, ALU.mult))
                c(V.tensor_tensor(z, z, var, ALU.mult))
                c(V.tensor_scalar(z, z, -0.5, 1.5, ALU.mult, ALU.add))
                c(V.tensor_tensor(y, y, z, ALU.mult))
                c(V.tensor_tensor(by_tile(centred), by_tile(centred),
                                  y.unsqueeze(2).to_broadcast((P, NT, D)), ALU.mult))
                V.tensor_scalar(out, by_tile(centred), 0.0, None, ALU.max).then_inc(L.h_made, 1)
                dve.wait_ge(L.h_made, 1)

            def make_table(L, c):
                for q in range(NT // 4):
                    dve.wait_ge(L.rows_ps, q + 1)
                    if L.n == 0:
                        V.tensor_copy(table3[:, 4 * q:4 * q + 4, :],
                                      rows_ps[q % 2][:, 0:4 * R].rearrange("p (t r) -> p t r", r=R)
                                      ).then_inc(L.rows_made, 1)
                    else:
                        V.tensor_copy(table3[:, 4 * q:4 * q + 4, D:R],
                                      rows_ps[q % 2][:, 0:8].rearrange("p (t r) -> p t r", r=2)
                                      ).then_inc(L.rows_made, 1)
                dve.wait_ge(L.rows_made, NT // 4)
                c(V.tensor_scalar(s1s[:, :], table3[:, :, D + 1], ALPHA, None, ALU.mult))
                dve.wait_ge(L.mean_ps, 1)
                V.tensor_copy(mean_row[:, :], sum_ps[:, 0:D]).then_inc(L.mean_made, 1)
                dve.wait_ge(L.mean_made, 1)

            def extract():
                def take(cur, c):
                    rounds = sum(r for r, _ in cur.units)
                    dve.wait_ge(packs, cur.t * 2 + 2)
                    for r in range(rounds):
                        src = packed[cur.par] if r == 0 else words
                        c(V.scalar_tensor_tensor(
                            out=keys[:, :].bitcast(I32), in0=src[:, :].bitcast(I32), scalar=EXPONENT,
                            in1=word_no[:, :], op0=ALU.bitwise_and, op1=ALU.bitwise_or))
                        gate(dve)
                        best = found[:, 8 * r:8 * r + 8]
                        c(V.max(best, keys[:, :]))
                        if r < rounds - 1:
                            gate(dve)
                            c(V.match_replace(kept[:, :], best, keys[:, :], 0.0))
                            c(V.tensor_tensor(taken[:, :], keys[:, :], kept[:, :], ALU.subtract))
                            c(V.tensor_scalar(taken[:, :].bitcast(I32), taken[:, :].bitcast(I32),
                                              EXPONENT, None, ALU.bitwise_and))
                            c(V.tensor_tensor(words[:, :], src[:, :], taken[:, :], ALU.subtract))
                    n = cur.slots
                    for r in range(rounds):
                        best = ranked[:, 8 * r:8 * r + 8]
                        gate(dve)
                        c(V.max(best, found[:, 0:n]))
                        if r < rounds - 1:
                            gate(dve)
                            c(V.match_replace(found[:, 0:n], best, found[:, 0:n], 0.0))
                    c.inc(V.tensor_scalar(exponent[:, 0:n], ranked[:, 0:n].bitcast(I32), 23, None,
                                          ALU.logical_shift_right))
                    c(V.tensor_scalar(word_of[:, 0:n], ranked[:, 0:n].bitcast(I32), WORDS - 1, None,
                                      ALU.bitwise_and))
                    c(V.tensor_scalar(bit1[:, 0:n], exponent[:, 0:n], 126.0, 0.0, ALU.subtract, ALU.max))
                    k = 0
                    for u, (r, _) in enumerate(cur.units):
                        c.inc(V.tensor_scalar(valid[:, k:k + 8 * r], bit1[:, k:k + 8 * r], 0.5, None,
                                              ALU.is_ge, ALU.add, accum_out=count[:, u:u + 1]))
                        k += 8 * r
                    c.wait()
                    pairs = values[cur.par][:, 0:2 * n].rearrange("p (k v) -> p k v", v=2)
                    c.inc(V.tensor_tensor(pairs[:, :, 0], word_of[:, 0:n], valid[:, 0:n], ALU.mult))
                    c.inc(V.tensor_copy(pairs[:, :, 1], bit1[:, 0:n]))
                    nu = len(cur.units)
                    c.inc(V.tensor_copy(count16[cur.par][:, 0:nu], count[:, 0:nu]))
                    total = count[:, 0:1]
                    if nu > 1:
                        total = first[:, 0:1]
                        c(V.tensor_reduce(total, count[:, 0:nu], AX.X, ALU.add))
                    d = degree[cur.par]
                    V.scalar_tensor_tensor(out=col(missed, cur.t), in0=d[:, 0:1], scalar=d[:, 1:2],
                                           in1=total, op0=ALU.add, op1=ALU.subtract
                                           ).then_inc(counted, 1)
                    dve.wait_ge(counted, cur.t + 1)

                def index_of(prev, c):
                    dve.wait_ge(edged, prev.unit + len(prev.units))
                    e = edges_ps[:, 64 * prev.par:64 * prev.par + 2 * prev.chunks
                                 ].rearrange("p (c v) -> p c v", v=2)
                    c(V.tensor_scalar(edge_f[:, 0:prev.chunks], e[:, :, 1], float(WORDS), float(-WORDS),
                                      ALU.mult, ALU.add))
                    c(V.tensor_tensor(edge_f[:, 0:prev.chunks], edge_f[:, 0:prev.chunks], e[:, :, 0],
                                      ALU.add))
                    V.tensor_scalar(col(index_all, prev.chunk, prev.chunks), edge_f[:, 0:prev.chunks],
                                    0.0, None, ALU.max).then_inc(indexed, 1)

                def place_of(cur, c):
                    nu = len(cur.units)
                    dve.wait_ge(based, cur.t + 1)
                    base = starts_ps[:, 0:nu]
                    c.inc(V.tensor_copy(first[:, 0:nu], base))
                    c(V.tensor_scalar(start_m[:, 0:nu], base, -1.0, 0.5, ALU.mult, ALU.add))
                    c.inc(V.scalar_tensor_tensor(out=col(middle, cur.unit, nu), in0=count[:, 0:nu],
                                                 scalar=-0.5, in1=start_m[:, 0:nu], op0=ALU.mult,
                                                 op1=ALU.add))
                    c.inc(V.tensor_scalar(col(reach, cur.unit, nu), count[:, 0:nu], 0.5, -0.25,
                                          ALU.mult, ALU.add))
                    for u, (r, chunks) in enumerate(cur.units):
                        c.inc(V.tensor_scalar(col(beyond, cur.unit + u), count[:, u:u + 1],
                                              first[:, u:u + 1], float(chunks * P), ALU.add,
                                              ALU.subtract))
                        if cur.static or u:
                            dve.wait_ge(edged, cur.unit + u)
                        V.tensor_scalar(place[:, 0:8 * r + chunks * P],
                                        edge_no[:, SHIFT - 8 * r:SHIFT + chunks * P],
                                        first[:, u:u + 1], None, ALU.is_equal).then_inc(placed, 1)

                def step(cur, prev):
                    if cur:
                        c = Steps(dve, dve_x, cur.extract_step)
                        take(cur, c)
                    else:
                        c = Steps(dve, dve_x, sum(extract_steps(t) for t in range(NT)))
                    if prev:
                        index_of(prev, c)
                    if cur:
                        place_of(cur, c)
                        assert c.n == extract_steps(cur.static), (cur.static, c.n)

                each_tile(dve, NT, step)

            def judge():
                c = Steps(dve, dve_f)
                dve.wait_ge(counted, NT)
                dve.wait_ge(placed, NU)
                c.inc(V.tensor_reduce(fault[:, 0:1], missed[:, :], AX.X, ALU.max,
                                      apply_absolute_value=True))
                c.inc(V.tensor_reduce(fault[:, 1:2], beyond[:, :], AX.X, ALU.max))
                c(V.memset(fault[:, 3:4], 1.0))
                V.tensor_scalar(fault[:, 2:3], fault[:, 0:1], fault[:, 1:2], 0.0, ALU.max, ALU.is_gt
                                ).then_inc(fault_made, 1)
                dve.wait_ge(fault_sum, 1)
                V.tensor_scalar(flag[0:1, 0:1], edges_ps[0:1, 256:257], 0.0, None, ALU.is_gt
                                ).then_inc(flag_made, 1)
                dve.wait_ge(flag_made, 1)

            def attend(L):
                def scores(cur, c):
                    s1 = table3[:, bass.ds(cur.t, 1), D + 1]
                    sc = scores_of(cur)
                    for k, (u, c0, e0, nc_) in enumerate(cur.segments):
                        g, w = cur.segment + k, nc_ * P
                        dve.wait_ge(L.distance_made, g + 1)
                        c.inc(V.tensor_scalar(mask[:, 0:w], mask[:, 0:w], col(reach, cur.unit + u),
                                              MASKED, ALU.is_gt, ALU.mult))
                        dve.wait_ge(L.slope_made, g + 1)
                        V.scalar_tensor_tensor(out=leaky[:, 0:w], in0=s2_ps[:, 0:w], scalar=s1,
                                               in1=slope[:, 0:w], op0=ALU.add, op1=ALU.max
                                               ).then_inc(L.s2_read, 1)
                        if k == 0 and cur.static >= 2:
                            dve.wait_ge(L.group_summed, groups_before(cur))
                            gate(dve)
                        dve.wait_ge(L.s2_read, g + 1)
                        c.wait()
                        gate(dve)
                        V.tensor_tensor_reduce(
                            out=sc[:, c0 * P:c0 * P + w], in0=leaky[:, 0:w], in1=mask[:, 0:w],
                            scale=1.0, scalar=FLOOR, op0=ALU.add, op1=ALU.max,
                            accum_out=top[:, k:k + 1]).then_inc(L.masked, 1)
                    dve.wait_ge(L.masked, cur.segment + len(cur.segments))
                    m = top[:, 0:1]
                    if len(cur.segments) > 1:
                        m = top[:, 7:8]
                        c(V.tensor_reduce(m, top[:, 0:len(cur.segments)], AX.X, ALU.max))
                    V.tensor_scalar(shift[cur.par][:, :], m, -1.0, None, ALU.mult
                                    ).then_inc(L.shifted, 1)

                def finish(prev):
                    dve.wait_ge(L.group_summed, prev.group + prev.groups)
                    V.tensor_copy(agg3[:, bass.ds(prev.t, 1), :],
                                  sum_ps[:, D * prev.par:D * prev.par + D].unsqueeze(1))
                    V.tensor_copy(col(den_all, prev.t), den[prev.par][:, :]).then_inc(L.finished, 1)

                def step(cur, prev):
                    if cur:
                        c = Steps(dve, L.dve, cur.score_step)
                        scores(cur, c)
                        assert c.n == score_steps(cur.static), (cur.static, c.n)
                    if prev:
                        finish(prev)

                each_tile(dve, NT, step)
                dve.wait_ge(L.finished, NT)

            def dense_attend(L):
                BLK = SEG * P
                dve.wait_ge(L.d_s2, 32)
                per_tile = 1 + 3 * (N // BLK) + 1 + 2
                with dve.Fori(0, NT) as i:
                    c = Steps(dve, L.d_dve, i * per_tile)
                    dve.wait_ge(L.d_in, i * 16 + 16)
                    c(V.tensor_scalar(dense_scores, adj[0][:, :], 0.0, MASKED, ALU.is_le, ALU.mult))
                    for k in range(N // BLK):
                        at = slice(k * BLK, (k + 1) * BLK)
                        c(V.tensor_scalar(slope[:, :], s2_row[:, at],
                                          table3[:, bass.ds(i, 1), D + 1], None, ALU.add))
                        c(V.scalar_tensor_tensor(out=leaky[:, :], in0=slope[:, :], scalar=ALPHA,
                                                 in1=slope[:, :], op0=ALU.mult, op1=ALU.max))
                        gate(dve)
                        c(V.tensor_tensor_reduce(
                            out=dense_scores[:, at], in0=leaky[:, :], in1=dense_scores[:, at],
                            scale=1.0, scalar=FLOOR, op0=ALU.add, op1=ALU.max,
                            accum_out=top[:, k:k + 1]))
                    c(V.tensor_reduce(mask[:, 0:1], top[:, 0:N // BLK], AX.X, ALU.max))
                    V.tensor_scalar(shift[0][:, :], mask[:, 0:1], -1.0, None, ALU.mult
                                    ).then_inc(L.d_shift, 1)
                    for q in range(NT // 4):
                        dve.wait_ge(L.d_turned, i * (NT // 4) + q + 1)
                        V.tensor_copy(probsT[0][:, :], turned_ps[:, :]).then_inc(L.d_copied, 1)
                    dve.wait_ge(L.d_summed, i + 1)
                    c.inc(V.tensor_copy(agg3[:, bass.ds(i, 1), :], sum_ps[:, 0:D].unsqueeze(1)))
                    c.inc(V.tensor_copy(col(den_all, i), den[0][:, :]))
                    c.wait()
                    dve.sem_inc(L.d_done, 1)
                    assert c.n == per_tile, c.n

            def divide(L, c):
                none, rec = stat[:, 0:NT], stat[:, NT:2 * NT]
                c(V.tensor_scalar(none, den_all[:, :], 0.5, None, ALU.is_lt))
                c(V.tensor_tensor(rec, den_all[:, :], none, ALU.add))
                c(V.reciprocal(rec, rec))
                wide = (P, NT, D)
                c(V.tensor_tensor(agg3, agg3, rec.unsqueeze(2).to_broadcast(wide), ALU.mult))
                c(V.tensor_tensor(by_tile(exp_b), none.unsqueeze(2).to_broadcast(wide),
                                  mean_row[:, :].unsqueeze(1).to_broadcast(wide), ALU.mult))
                c(V.tensor_tensor(agg[:, :], agg[:, :], exp_b, ALU.add))

            make_consts()
            c0 = Steps(dve, sem("dve_table0_step"))
            dve.wait_ge(x_in, 16)
            normalise(layers[0], c0, agg[:, :], agg[:, :], table[:, 0:SZ], agg3)
            make_table(layers[0], c0)
            extract()
            judge()
            dense = dve.value_load(flag[0:1, 0:1], min_val=0, max_val=1)
            for L in layers:
                with dve.If(dense > 0):
                    dense_attend(L)
                with dve.If(dense < 1):
                    attend(L)
                c = Steps(dve, L.post)
                divide(L, c)
                dve.wait_ge(L.x_in, 16)
                if L.n == 0:
                    V.tensor_scalar(exp_b, agg[:, :], 0.0, None, ALU.min).then_inc(L.neg_made, 1)
                    dve.wait_ge(L.exp_made, 1)
                    c(V.scalar_tensor_tensor(out=agg[:, :], in0=exp_b, scalar=-1.0, in1=agg[:, :],
                                             op0=ALU.add, op1=ALU.max))
                    c(V.tensor_tensor(agg[:, :], agg[:, :], x_b, ALU.add))
                    dve.sem_inc(L.x_out, 1)
                    normalise(layers[1], c, agg[:, :], centred_b, square_b, table3[:, :, 0:D])
                    make_table(layers[1], c)
                    dve.wait_ge(L.x_in, 32)
                else:
                    V.scalar_tensor_tensor(out=agg[:, :], in0=agg[:, :], scalar=0.0, in1=x_b,
                                           op0=ALU.max, op1=ALU.add).then_inc(L.x_out, 1)

        @block.tensor
        def _(pe):
            T = nc.tensor

            def make_table(L):
                rhs = a_sb[:, 2:4]
                if L.n == 0:
                    rhs = w_sb[:, :]
                    pe.wait_ge(consts, 6)
                    pe.wait_ge(w_in, 5 * 16)
                    pe.wait_ge(dve_c, 5 + BITS)
                    T.transpose(sum_ps[0:D, 0:D], w_sb[:, 0:D], identity[0:D, 0:D]).then_inc(L.wT_ps, 1)
                    pe.wait_ge(L.wT_made, 1)
                    T.matmul(sum_ps[0:D, 64:66], wT[:, :], a_sb[:, 0:2], start=True, stop=True
                             ).then_inc(L.wa_ps, 1)
                    pe.wait_ge(L.wa_made, 1)
                pe.wait_ge(L.h_made, 1)
                n = R if L.n == 0 else 2

                def turn(q):
                    if q >= 2:
                        pe.wait_ge(L.hT_made, q - 1)
                    for k in range(4):
                        t = 4 * q + k
                        h = agg3[:, t, :] if L.n == 0 else table3[:, t, 0:D]
                        last = T.transpose(hT_ps[q % 2][0:D, k * P:(k + 1) * P], h, identity[:, :])
                    last.then_inc(L.hT_ps, 1)

                turn(0)
                for q in range(NT // 4):
                    if q + 1 < NT // 4:
                        turn(q + 1)
                    pe.wait_ge(L.hT_made, q + 1)
                    if q >= 2:
                        pe.wait_ge(L.rows_made, q - 1)
                    for k in range(4):
                        last = T.matmul(rows_ps[q % 2][:, n * k:n * k + n], hT[q % 2][:, k * P:(k + 1) * P],
                                        rhs, start=True, stop=True)
                    last.then_inc(L.rows_ps, 1)
                pe.wait_ge(L.rows_made, NT // 4)
                for t in range(NT):
                    last = T.matmul(sum_ps[:, 0:D], mean_of[:, :], table3[:, t, 0:D], start=(t == 0),
                                    stop=(t == NT - 1))
                last.then_inc(L.mean_ps, 1)

            def pack():
                def words_of(cur, h):
                    pe.wait_ge(casts, cur.t * 2 + (h + 1))
                    if h == 0:
                        if cur.static >= 2:
                            pe.wait_ge(counted, cur.t - 1)
                        T.matmul(packed[cur.par][:, :], quarter[:, :], ones16[:, :], start=True, stop=False)
                    for b in range(BITS // 2):
                        bit = h * (BITS // 2) + b
                        last = T.matmul(packed[cur.par][:, :], weights[:, bit * P:(bit + 1) * P],
                                        signs[h][:, b * WORDS:(b + 1) * WORDS], start=False,
                                        stop=(bit == BITS - 1))
                    last.then_inc(packs, 1)

                def starts(prev):
                    pe.wait_ge(counted, prev.t + 1)
                    nu = len(prev.units)
                    T.matmul(starts_ps[:, 0:nu], before[:, :],
                             count16[prev.par][:, 0:nu], start=True, stop=True).then_inc(based, 1)

                def pack_edges(prev):
                    slot, chunk = 0, 0
                    for u, (r, chunks) in enumerate(prev.units):
                        pe.wait_ge(placed, prev.unit + (u + 1))
                        for c in range(chunks):
                            at = 64 * prev.par + 2 * (chunk + c)
                            for k in range(8 * r):
                                src = 8 * r - k + c * P
                                last = T.matmul(edges_ps[:, at:at + 2], place[:, src:src + P],
                                                values[prev.par][:, 2 * (slot + k):2 * (slot + k) + 2],
                                                start=(k == 0), stop=(k == 8 * r - 1))
                        last.then_inc(edged, 1)
                        slot += 8 * r
                        chunk += chunks

                def step(cur, prev):
                    if cur:
                        words_of(cur, 0)
                    if prev:
                        starts(prev)
                    if cur:
                        words_of(cur, 1)
                    if prev:
                        pack_edges(prev)

                each_tile(pe, NT, step)

            def attend(L):
                def front(cur):
                    pe.wait_ge(L.rows_in[cur.par], (cur.chunks_here + cur.chunks) * 16)
                    for k, (u, c0, e0, nc_) in enumerate(cur.segments):
                        g = cur.segment + k
                        if cur.static or k:
                            pe.wait_ge(L.s2T_made, g)
                        s2 = rows[cur.par][:, c0 * RG:(c0 + nc_) * RG
                                           ].rearrange("p (c r) -> p c r", r=RG)[:, :, D]
                        T.transpose(s2T_ps[0:nc_, 0:P], s2, identity[:, :]).then_inc(L.s2T_turned, 1)
                        pe.wait_ge(L.s2T_made, g + 1)
                        if cur.static or k:
                            pe.wait_ge(L.s2_read, g)
                        for c in range(nc_):
                            last = T.matmul(s2_ps[:, c * P:(c + 1) * P], select[0:nc_, c * P:(c + 1) * P],
                                            s2T[0:nc_, :], start=True, stop=True)
                        last.then_inc(L.s2_spread, 1)

                def back(prev):
                    pe.wait_ge(L.probs_made, prev.t + 1)
                    sc = scores_of(prev)
                    for k in range(prev.groups):
                        mine = range(4 * k, min(4 * k + 4, prev.chunks))
                        if prev.static or k:
                            pe.wait_ge(L.turned_copied, prev.group + k)
                        for c in mine:
                            last = T.transpose(turned_ps[:, (c % 4) * P:(c % 4 + 1) * P],
                                               sc[:, c * P:(c + 1) * P], identity[:, :])
                        last.then_inc(L.turned, 1)
                        pe.wait_ge(L.turned_copied, prev.group + (k + 1))
                        if k == 0 and prev.static:
                            pe.wait_ge(L.finished, prev.t)
                        for c in mine:
                            last = T.matmul(sum_ps[:, D * prev.par:D * prev.par + D],
                                            probsT[(prev.group0 + k) % 2][:, (c % 4) * P:(c % 4 + 1) * P],
                                            rows[prev.par][:, c * RG:c * RG + D], start=(c == 0),
                                            stop=(c == prev.chunks - 1))
                        last.then_inc(L.group_summed, 1)

                def step(cur, prev):
                    if cur:
                        front(cur)
                    if prev:
                        back(prev)

                pe.wait_ge(L.mean_made, 1)
                each_tile(pe, NT, step)

            def dense_attend(L):
                pe.wait_ge(L.mean_made, 1)
                with pe.Fori(0, NT) as i:
                    pe.wait_ge(L.d_probs, i + 1)
                    for q in range(NT // 4):
                        for k in range(4):
                            c = 4 * q + k
                            last = T.transpose(turned_ps[:, k * P:(k + 1) * P],
                                               dense_scores[:, c * P:(c + 1) * P], identity[:, :])
                        last.then_inc(L.d_turned, 1)
                        pe.wait_ge(L.d_copied, i * (NT // 4) + (q + 1))
                        for k in range(4):
                            c = 4 * q + k
                            last = T.matmul(sum_ps[:, 0:D], probsT[0][:, k * P:(k + 1) * P],
                                            table3[:, c, 0:D], start=(c == 0), stop=(c == NT - 1))
                    last.then_inc(L.d_summed, 1)

            make_table(layers[0])
            pack()
            pe.wait_ge(fault_made, 1)
            T.matmul(edges_ps[0:1, 256:257], fault[:, 2:3], fault[:, 3:4], start=True, stop=True
                     ).then_inc(fault_sum, 1)
            pe.wait_ge(flag_made, 1)
            dense = pe.value_load(flag[0:1, 0:1], min_val=0, max_val=1)
            for L in layers:
                with pe.If(dense > 0):
                    dense_attend(L)
                with pe.If(dense < 1):
                    attend(L)
                if L.n == 0:
                    make_table(layers[1])


_INS = ["x", "adj", "L0_gnn_W", "L0_gnn_a", "L1_gnn_a"]


def kernel(**inputs):
    import numpy as np
    import concourse.bacc as bacc
    from concourse.bass_utils import run_bass_kernel_spmd

    nc = bacc.Bacc("TRN2", target_bir_lowering=False, num_devices=1)
    arrays = {f"in_{name}": np.ascontiguousarray(inputs[name]) for name in _INS}
    aps = [nc.dram_tensor(name, a.shape, mybir.dt.from_np(a.dtype), kind="ExternalInput").ap()
           for name, a in arrays.items()]
    out = nc.dram_tensor("out", arrays["in_x"].shape, F32, kind="ExternalOutput").ap()
    gat_kernel(nc, *aps, out)
    return run_bass_kernel_spmd(nc, [arrays], core_ids=[0]).results[0]["out"]
```

```python
import concourse.bass as bass
from concourse import mybir
from contextlib import ExitStack

F32 = mybir.dt.float32
F16 = mybir.dt.float16
I32 = mybir.dt.int32
U32 = mybir.dt.uint32
I16 = mybir.dt.int16
ALU = mybir.AluOpType
ACT = mybir.ActivationFunctionType
AX = mybir.AxisListType

P = 128
ALPHA = 0.2
EPS = 1e-5
MASKED = -9.0e15
FLOOR = -1.0e15
BITS = 16
EXPONENT = 0x7F800000
OFFSET = 1 << 24
USED = -3.0e38
SEG = 4
RING = 4

HEAD_UNITS = [
    [(2, 16), (2, 4), (4, 2), (8, 1), (3, 1)], [(3, 8)], [(3, 6)], [(3, 6)],
    [(2, 5)], [(2, 5)], [(2, 4)], [(2, 4)],
]
TAIL_UNITS = [(2, 2)]
HEAD = len(HEAD_UNITS)
LEVELS0, LEVELS_HEAD, LEVELS_TAIL = 5, 4, 3


def units_of(t):
    return HEAD_UNITS[t] if t < HEAD else TAIL_UNITS


def levels_of(t):
    return LEVELS0 if t == 0 else LEVELS_HEAD if t < HEAD else LEVELS_TAIL


def chunks_of(t):
    return sum(c for _, c in units_of(t))


def groups_of(t):
    return -(-chunks_of(t) // 4)


def segments_of(t):
    out, at = [], 0
    for u, (_, c) in enumerate(units_of(t)):
        for k in range(0, c, SEG):
            out.append((u, at + k, k * P, min(SEG, c - k)))
        at += c
    return out


def word_rounds_of(t):
    return sum(r for r, _ in (units_of(t)[:-1] if t == 0 else units_of(t)))


def take_steps(t):
    rounds, units, levels = word_rounds_of(t), len(units_of(t)), levels_of(t)
    best = 2 * units_of(t)[-1][0] - 1
    return 2 * rounds + 5 + 3 * levels - 2 + 1 + best + 4 + units + (units > 1)


def score_steps(t):
    return len(segments_of(t)) + (len(segments_of(t)) > 1)


class Tile:

    def __init__(self, t, i=0):
        def so_far(of, tiles=None, per_turn=RING):
            return sum(of(k) for k in (range(t) if tiles is None else tiles)) + i * (per_turn * of(t))

        self.static, self.t = t, i * RING + t
        self.par, self.ring = t % 2, t % RING
        self.pair = i * (RING // 2) + t // 2
        self.units, self.chunks, self.groups = units_of(t), chunks_of(t), groups_of(t)
        self.segments, self.levels = segments_of(t), levels_of(t)
        self.slots = 8 * sum(r for r, _ in self.units)
        self.chunk = so_far(chunks_of)
        self.unit = so_far(lambda k: len(units_of(k)))
        self.segment = so_far(lambda k: len(segments_of(k)))
        self.group = so_far(groups_of)
        self.group_static = sum(groups_of(k) for k in range(t))
        self.ring_chunks = so_far(chunks_of, range(t % RING, t, RING), 1)
        self.take_step = so_far(take_steps)
        self.score_step = so_far(score_steps)

    def groups_until(self, back):
        return self.group - sum(groups_of(k) for k in range(self.static - back + 1, self.static))


class Window:

    def __init__(self, s, i, tiles):
        self.s, self.i, self.tiles = s, i, tiles

    def back(self, k):
        return Tile(self.s - k, self.i) if 0 <= self.s - k < self.tiles else None


def each_step(eng, tiles, lag, step, start=0):
    first = -(-(HEAD + lag) // RING) * RING
    for s in range(start, first):
        step(Window(s, 0, tiles))
    with eng.Fori(0, (tiles - first) // RING) as i:
        for s in range(first, first + RING):
            step(Window(s, i, tiles))
    for s in range(tiles, tiles + lag):
        step(Window(s, 0, tiles))


def gat_kernel(nc, x_d, adj_d, w_d, a0_d, a1_d, out_d):
    N, D = x_d.shape
    NT = N // P
    WORDS = N // BITS
    HALF = N // 2
    TAIL = NT - HEAD
    NCH = sum(chunks_of(t) for t in range(NT))
    NU = sum(len(units_of(t)) for t in range(NT))
    C0 = chunks_of(0)
    CMAX = max(chunks_of(t) for t in range(1, NT))
    KMAX = max(8 * r for t in range(NT) for r, _ in units_of(t))
    EMAX = P * max(c for t in range(NT) for _, c in units_of(t))
    SLOTS = Tile(0).slots
    BELOW = max((levels_of(0) - 1) * 8 * word_rounds_of(0),
                max(levels_of(t) * 8 * word_rounds_of(t) for t in range(1, NT)))
    R = D + 2
    RG = D + 1
    SZ = NT * D
    PIECES = 4
    PT = NT // PIECES

    table_d = [nc.dram_tensor(f"table{n}", (N, RG), F32, kind="Internal").ap() for n in range(2)]
    s2_d = [nc.dram_tensor(f"s2_{n}", (N, 1), F32, kind="Internal").ap() for n in range(2)]
    x1_d = nc.dram_tensor("x1_scratch", (P, SZ), F32, kind="Internal").ap()

    ctx = ExitStack()
    with ctx:
        def sb(name, shape, dt=F32):
            return ctx.enter_context(nc.sbuf_tensor(name, shape, dt))

        def sem(name):
            return ctx.enter_context(nc.semaphore(name))

        def by_tile(ap, width=D):
            return ap.rearrange("p (t d) -> p t d", d=width)

        adj = [sb(f"adj{b}", [P, N], I32) for b in range(2)]
        signs = [sb(f"signs{b}", [P, HALF], F16) for b in range(2)]
        table = sb("table", [P, NT * R])
        table3 = by_tile(table[:, :], R)
        x_all = sb("x_all", [P, SZ])
        x3 = by_tile(x_all[:, :])
        agg = sb("agg", [P, SZ])
        agg3 = by_tile(agg[:, :])
        big_scores = agg[:, SZ - C0 * P:SZ]

        identity = sb("identity", [P, P])
        weights = sb("weights", [P, BITS * P], F16)
        before = sb("before", [P, P])
        halves, quarters = (sb(n, [P, len(HEAD_UNITS[0])]) for n in ("halves", "quarters"))
        mean_of = sb("mean_of", [P, P])
        word_no = sb("word_no", [P, WORDS])
        edge_no = sb("edge_no", [P, KMAX + EMAX], I16)
        select = sb("select", [SEG, SEG * P])
        room = sb("room", [P, NU])
        eps = sb("eps", [P, 1])

        keys = sb("keys", [P, WORDS])
        kept = sb("kept", [P, WORDS])
        found = sb("found", [P, 8 * word_rounds_of(0)])
        found_i = sb("found_i", [P, 8 * word_rounds_of(0)], I32)
        word_of = sb("word_of", [P, 8 * word_rounds_of(0)], I32)
        bits_i = sb("bits_i", [P, 8 * word_rounds_of(0)], I32)
        bits = sb("bits", [P, 8 * word_rounds_of(0)])
        top_bit = sb("top_bit", [P, 8 * word_rounds_of(0)])
        lower = sb("lower", [P, BELOW])
        ranked = sb("ranked", [P, SLOTS])
        exponent = sb("exponent", [P, SLOTS], I32)
        column = sb("column", [P, SLOTS], I32)
        valid = sb("valid", [P, SLOTS])
        values = [sb(f"values{b}", [P, 2 * SLOTS], F16) for b in range(2)]
        degree = [sb(f"degree{b}", [P, 2]) for b in range(2)]
        total = sb("total", [P, 1])
        place = sb("place", [P, KMAX + EMAX], F16)
        edge_f = sb("edge_f", [P, C0])
        missed = sb("missed", [P, NT])
        count_all = sb("count_all", [P, NU])
        first_all = sb("first_all", [P, NU])
        middle = sb("middle", [P, NU])
        half_count = sb("half_count", [P, NU])
        reach = sb("reach", [P, NU])
        index_all = sb("index_all", [P, NCH], U32)
        fault = sb("fault", [P, 4])
        flag = sb("flag", [1, 1], I32)

        index = [sb(f"index{r}", [P, C0 if r == 0 else CMAX], U32) for r in range(RING)]
        rows = [sb(f"rows{r}", [P, (C0 if r == 0 else CMAX) * RG]) for r in range(RING)]
        s2T = sb("s2T", [SEG, P])
        slope = sb("slope", [P, SEG * P])
        mask = sb("mask", [P, SEG * P])
        leaky = sb("leaky", [P, SEG * P])
        scores = [sb(f"scores{b}", [P, CMAX * P]) for b in range(2)]
        top = sb("top", [P, 8])
        shift = [sb(f"shift{b}", [P, 1]) for b in range(2)]
        den = sb("den", [P, RING])
        no_edge = sb("no_edge", [P, 2])
        rec = sb("rec", [P, 2])
        acc = sb("acc", [P, RING * D])
        acc3 = by_tile(acc[:, :])
        probsT = [sb(f"probsT{b}", [P, 512]) for b in range(2)]
        s1 = [sb(f"s1_{n}", [P, NT]) for n in range(2)]
        s1_slope = [sb(f"s1_slope{n}", [P, NT]) for n in range(2)]
        mean_row = [sb(f"mean_row{n}", [P, D]) for n in range(2)]

        pair_a, pair_b = sb("pair_a", [P, 2 * D]), sb("pair_b", [P, 2 * D])
        pair_h = sb("pair_h", [P, 2 * D])
        pair_s = sb("pair_s", [P, 4])
        root2 = [sb(f"root2_{b}", [P, 2]) for b in range(2)]
        stats = sb("stats", [P, 2 * 6])
        aggr = [sb(f"aggr{b}", [P, 4]) for b in range(2)]
        h_sum = sb("h_sum", [P, 2 * D])
        dots = sb("dots", [P, D])
        a_row = sb("a_row", [P, 2 * D])

        stat = sb("stat", [P, 5 * NT])
        den_all = sb("den_all", [P, NT])
        w_sb = sb("w_sb", [D, R])
        wT = sb("wT", [D, D])
        a_sb = sb("a_sb", [D, 4])
        hT = [sb(f"hT{b}", [D, 4 * P]) for b in range(2)]

        bufs = [adj[b][:, k * SZ:(k + 1) * SZ].bitcast(F32) for b in range(2) for k in range(2)]
        x_b, exp_b, centred_b, square_b = bufs
        s2_row = adj[1][:, :].bitcast(F32)
        dense_scores = adj[0][:, :].bitcast(F32)

        def ps(name, shape):
            return ctx.enter_context(nc.psum_tensor(name, shape, F32))

        packed = [ps(f"packed{b}", [P, WORDS]) for b in range(2)]
        starts_ps, edges_ps, s2T_ps = ps("starts_ps", [P, 512]), ps("edges_ps", [P, 512]), ps("s2T_ps", [P, 512])
        s2_ps, turned_ps, sum_ps = ps("s2_ps", [P, 512]), ps("turned_ps", [P, 512]), ps("sum_ps", [P, 512])
        hT_ps = [turned_ps, s2T_ps]
        rows_ps = [s2_ps, edges_ps]

        consts, dve_c = sem("consts_made"), sem("dve_const_step")
        x_in, w_in, x_again = sem("x_in"), sem("w_in"), sem("x_again")
        adj_in = [sem(f"adj_in{b}") for b in range(2)]
        casts, packs, counted = sem("signs_made"), sem("halves_packed"), sem("edges_counted")
        summed, placed, edged = sem("starts_summed"), sem("places_made"), sem("edges_packed")
        indexed, firsts = sem("indices_made"), sem("firsts_copied")
        dve_t, dve_i, dve_f = sem("dve_take_step"), sem("dve_index_step"), sem("dve_fault_step")
        fault_made, fault_sum, flag_made = sem("fault_made"), sem("fault_summed"), sem("flag_made")
        gates = sem("gate")
        recs, den_used, neg_made, exp_made = sem("recs_made"), sem("sums_used"), sem("neg_made"), sem("exp_made")
        x1_made, var_made, root_made, h_made = sem("x1_made"), sem("var_made"), sem("root_made"), sem("h_made")
        row_made, pair_out = sem("pair_rows_made"), sem("pair_rows_stored")
        pool_1, pool_2, pool_3 = sem("pool_sum_step"), sem("pool_x_step"), sem("pool_h_step")
        dve_r, dve_v, dve_d, act_r = sem("dve_rec_step"), sem("dve_var_step"), sem("dve_dot_step"), sem("act_root_step")
        h_mean, h_total, s1_made, out_pairs, out_in = (sem("h_mean_summed"), sem("h_mean_made"), sem("s1_slope_made"),
                                                       sem("out_pairs_made"), sem("out_stored"))
        pool_m = sem("reach_made")

        class Table:

            def __init__(self, n):
                def s(name):
                    return sem(f"{name}_t{n}")
                self.n, self.layer = n, {0: 0, 2: 0, 3: 1}[n]
                self.step, self.act, self.var, self.root, self.h = (
                    s("dve_step"), s("act_step"), s("var_made"), s("root_made"), s("h_made"))
                self.wT_ps, self.wT, self.wa_ps, self.wa = s("wT_ps"), s("wT"), s("wa_ps"), s("wa")
                self.hT_ps, self.hT, self.rows_ps, self.rows = s("hT_ps"), s("hT"), s("rows_ps"), s("rows")
                self.mean_ps, self.mean, self.stored = s("mean_ps"), s("mean"), s("stored")

        class Attention:

            def __init__(self, n):
                def s(name):
                    self.signals.append(sem(f"{name}_{n}"))
                    return self.signals[-1]
                self.n, self.signals = n, []
                self.index_copied, self.rows_in = s("index_copied"), [s(f"rows_in{r}") for r in range(RING)]
                self.s2T_turned, self.s2T_made, self.s2_spread = s("s2T_turned"), s("s2T_made"), s("s2_spread")
                self.slope_made, self.distance_made, self.s2_read = (
                    s("slope_made"), s("distance_made"), s("s2_read"))
                self.masked, self.dve, self.shifted, self.probs = (
                    s("masked"), s("dve_score_step"), s("shifted"), s("probs_made"))
                self.turned, self.turned_copied, self.group_summed = (
                    s("turned"), s("turned_copied"), s("group_summed"))
                self.copied = s("sums_copied")

        class Dense:

            def __init__(self, n, spare=None):
                def s(name):
                    return spare.signals.pop() if spare else sem(f"dense_{name}_{n}")
                self.n = n
                self.s2, self.adj, self.dve, self.shifted, self.probs = (
                    s("s2"), s("adj_in"), s("dve_step"), s("shifted"), s("probs"))
                self.turned, self.copied, self.summed, self.done = s("turned"), s("copied"), s("summed"), s("done")
                self.post, self.neg, self.exp, self.x_in, self.x_out = s("post"), s("neg"), s("exp"), s("x_in"), s("x_out")

        first_table, dense_tables = Table(0), [Table(2), Table(3)]
        layers = [Attention(0), Attention(1)]
        dense_layers = [Dense(0, layers[1]), Dense(1)]

        block = ctx.enter_context(nc.Block())

        class Steps:

            def __init__(self, eng, s, base=0, gated=False):
                self.eng, self.s, self.base, self.n, self.gated = eng, s, base, 0, gated

            def inc(self, ins):
                self.n += 1
                ins.then_inc(self.s, 1)

            def wait(self):
                self.eng.wait_ge(self.s, self.base + self.n)
                if self.gated:
                    gate(self.eng)

            def __call__(self, ins):
                self.inc(ins)
                self.wait()

        def gate(eng):
            eng.sem_inc(gates, 1)

        def col(ap, at, n=1):
            return ap[:, bass.ds(at, n)]

        def tiles_of(ap3, t, n=1):
            return ap3[:, bass.ds(t, n), :]

        def head_of(ap):
            return ap[0:HEAD * P, :].rearrange("(t p) d -> p t d", p=P)

        def tail_of(ap):
            return ap[HEAD * P:N, :].rearrange("(p t) d -> p t d", p=P)

        adj_head = adj_d[0:HEAD * P, :].rearrange("(t p) n -> t p n", p=P)
        adj_tail = adj_d[HEAD * P:N, :].rearrange("(p t) n -> t p n", p=P)

        def rows_dma(eng, to_dram, ap_d, ap3, s):
            for part, view in ((slice(0, HEAD), head_of(ap_d)), (slice(HEAD, NT), tail_of(ap_d))):
                a, b = (view, ap3[:, part, :]) if to_dram else (ap3[:, part, :], view)
                eng.dma_start(a, b).then_inc(s, 16)

        def scores_of(tile):
            return big_scores if tile.static == 0 else scores[tile.par][:, 0:tile.chunks * P]

        def place_of_group(tile, k):
            return (range(4 * k, min(4 * k + 4, tile.chunks)), probsT[(tile.group_static + k) % 2])

        @block.sync
        def _(sp):
            def load_tile(w):
                cur = w.back(0)
                if cur:
                    if cur.static >= 2:
                        sp.wait_ge(casts, cur.t * 2 - 2)
                    src = adj_head[w.s] if w.s < HEAD else adj_tail[w.i * RING + (w.s - HEAD)]
                    sp.dma_start(adj[cur.par][:, :], src).then_inc(adj_in[cur.par], 16)
                done = w.back(16)
                if done and w.s % 2 == 0:
                    sp.wait_ge(row_made, done.pair + 1)
                    src = table3[:, bass.ds(done.t, 2), 0:RG]
                    if done.static < HEAD:
                        dst = head_of(table_d[1])[:, done.static:done.static + 2, :]
                    else:
                        dst = tail_of(table_d[1])[:, bass.ds(w.i * RING + (done.static - HEAD), 2), :]
                    sp.dma_start(dst, src).then_inc(pair_out, 16)

            def dense_loads(L, B):
                sp.wait_ge(B.rows, NT // 4)
                with nc.allow_non_contiguous_dma(reason="one column, on the dense path alone"):
                    rows_dma(sp, True, s2_d[L.n], table3[:, :, D:D + 1], L.s2)
                sp.wait_ge(L.s2, 32)
                sp.dma_start(s2_row, s2_d[L.n].rearrange("n one -> one n").to_broadcast((P, N))
                             ).then_inc(L.s2, 16)
                for t in range(HEAD):
                    if t:
                        sp.wait_ge(L.done, t)
                    sp.dma_start(adj[0][:, :], adj_head[t]).then_inc(L.adj, 16)
                with sp.Fori(0, TAIL) as i:
                    sp.wait_ge(L.done, i + HEAD)
                    sp.dma_start(adj[0][:, :], adj_tail[i]).then_inc(L.adj, 16)

            rows_dma(sp, False, x_d, x3, x_in)
            sp.dma_start(w_sb[:, 0:D], w_d).then_inc(w_in, 16)
            for n, a_d in enumerate((a0_d, a1_d)):
                sp.dma_start(a_sb[:, 2 * n:2 * n + 1], a_d[D:2 * D, :]).then_inc(w_in, 16)
                sp.dma_start(a_sb[:, 2 * n + 1:2 * n + 2], a_d[0:D, :]).then_inc(w_in, 16)
            sp.dma_start(a_row[:, :], a1_d.rearrange("n one -> one n").to_broadcast((P, 2 * D))
                         ).then_inc(w_in, 16)

            def step(w):
                load_tile(w)
                if w.s == 2:
                    sp.wait_ge(first_table.rows, NT // 4)
                    rows_dma(sp, True, table_d[0], table3[:, :, 0:RG], first_table.stored)

            each_step(sp, NT, 16, step)
            sp.wait_ge(pair_out, NT // 2 * 16)
            sp.wait_ge(flag_made, 1)
            dense = sp.value_load(flag[0:1, 0:1], min_val=0, max_val=1)
            with sp.If(dense < 1):
                def store(w):
                    done = w.back(3)
                    if done and w.s % RING == RING - 1:
                        sp.wait_ge(out_pairs, done.pair + 2)
                        src = x3[:, bass.ds(done.t, RING), :]
                        if done.static < HEAD:
                            dst = head_of(out_d)[:, done.static:done.static + RING, :]
                        else:
                            dst = tail_of(out_d)[:, bass.ds(w.i * RING + (done.static - HEAD), RING), :]
                        sp.dma_start(dst, src).then_inc(out_in, 16)

                each_step(sp, NT, 3, store)
                sp.wait_ge(out_in, NT // RING * 16)
            with sp.If(dense > 0):
                rows_dma(sp, False, x_d, x3, x_again)
                for L, B in zip(dense_layers, dense_tables):
                    dense_loads(L, B)
                    sp.wait_ge(L.post, 1)
                    if L.n == 0:
                        rows_dma(sp, False, x_d, by_tile(x_b), L.x_in)
                        sp.wait_ge(L.x_out, 1)
                        sp.dma_start(x1_d, agg[:, :]).then_inc(L.x_in, 16)
                        sp.wait_ge(L.x_in, 48)
                    else:
                        sp.dma_start(x_b, x1_d).then_inc(L.x_in, 16)
                        sp.wait_ge(L.x_out, 1)
                        rows_dma(sp, True, out_d, agg3, L.x_in)
                        sp.wait_ge(L.x_in, 48)

        @block.gpsimd
        def _(pool):
            G = nc.gpsimd

            def make_consts():
                G.memset(identity[:, :], 0.0).then_inc(consts, 1)
                G.memset(before[:, :], 1.0).then_inc(consts, 1)
                pool.wait_ge(consts, 2)
                G.affine_select(out=identity[:, :], in_=identity[:, :], compare_op=ALU.not_equal, fill=1.0,
                                base=0, pattern=[[-1, P]], channel_multiplier=1).then_inc(consts, 1)
                G.affine_select(out=before[:, :], in_=before[:, :], compare_op=ALU.is_gt, fill=0.0,
                                base=0, pattern=[[1, P]], channel_multiplier=-1).then_inc(consts, 1)
                G.iota(word_no[:, :], [[1, WORDS]], base=-OFFSET, channel_multiplier=0,
                       allow_small_or_imprecise_dtypes=True).then_inc(consts, 1)
                G.iota(edge_no[:, :], [[1, KMAX + EMAX]], base=-KMAX, channel_multiplier=0,
                       allow_small_or_imprecise_dtypes=True).then_inc(consts, 1)
                G.memset(h_sum[:, :], 0.0).then_inc(consts, 1)
                G.memset(halves[:, :], 0.5).then_inc(consts, 1)
                G.memset(quarters[:, :], 0.25).then_inc(consts, 1)

            def gather(L, cur):
                if cur.static >= RING:
                    pool.wait_ge(L.group_summed, cur.groups_until(RING))
                G.tensor_copy(index[cur.ring][:, 0:cur.chunks], col(index_all, cur.chunk, cur.chunks)
                              ).then_inc(L.index_copied, 1)
                pool.wait_ge(L.index_copied, cur.t + 1)
                gate(pool)
                for c in range(cur.chunks):
                    G.indirect_dma_start(
                        rows[cur.ring][:, c * RG:(c + 1) * RG], None, table_d[L.n],
                        bass.IndirectOffsetOnAxis(ap=index[cur.ring][:, c:c + 1], axis=0)
                    ).then_inc(L.rows_in[cur.ring], 16)

            def reach_of(cur):
                n = len(cur.units)
                c = Steps(pool, pool_m, cur.t * 4, gated=True)
                count, first, half, mid, far = (
                    col(a, cur.unit, n) for a in (count_all, first_all, half_count, middle, reach))
                pool.wait_ge(firsts, cur.t + 1)
                gate(pool)
                c(G.tensor_tensor(half, count, halves[:, 0:n], ALU.mult))
                c.inc(G.tensor_tensor(far, half, quarters[:, 0:n], ALU.subtract))
                c(G.tensor_tensor(mid, halves[:, 0:n], half, ALU.subtract))
                c.inc(G.tensor_tensor(mid, mid, first, ALU.subtract))

            def sums(a):
                c = Steps(pool, pool_1, a.pair * 3, gated=True)
                wide = (P, 2, D)
                r = a.ring
                pool.wait_ge(recs, a.pair + 1)
                gate(pool)
                if a.static >= 2:
                    pool.wait_ge(x1_made, a.pair)
                    gate(pool)
                G.tensor_tensor(by_tile(pair_a[:, :]), acc3[:, r:r + 2, :],
                                rec[:, :].unsqueeze(2).to_broadcast(wide), ALU.mult).then_inc(pool_1, 1)
                G.tensor_tensor(by_tile(pair_b[:, :]), no_edge[:, :].unsqueeze(2).to_broadcast(wide),
                                mean_row[0][:, :].unsqueeze(1).to_broadcast(wide), ALU.mult
                                ).then_inc(pool_1, 1)
                c.n = 2
                c.wait()
                c(G.tensor_tensor(pair_a[:, :], pair_a[:, :], pair_b[:, :], ALU.add))
                G.tensor_scalar(pair_b[:, :], pair_a[:, :], 0.0, None, ALU.min).then_inc(neg_made, 1)

            def residual(a):
                c = Steps(pool, pool_2, a.pair * 3, gated=True)
                pool.wait_ge(exp_made, a.pair + 1)
                gate(pool)
                c.inc(G.tensor_scalar(pair_b[:, :], pair_b[:, :], -1.0, None, ALU.add))
                c(G.tensor_scalar(pair_a[:, :], pair_a[:, :], 0.0, None, ALU.max))
                c(G.tensor_tensor(pair_a[:, :], pair_a[:, :], pair_b[:, :], ALU.add))
                G.tensor_tensor(tiles_of(x3, a.t, 2), by_tile(pair_a[:, :]), tiles_of(x3, a.t, 2), ALU.add
                                ).then_inc(x1_made, 1)

            def normal(a):
                c = Steps(pool, pool_3, a.pair * 9, gated=True)
                v, z, wide = pair_s[:, 0:2], pair_s[:, 2:4], (P, 2, D)
                root = root2[a.ring // 2][:, :]
                mean, var = (aggr[a.ring // 2][:, :].rearrange("p (t v) -> p t v", v=2)[:, :, k] for k in range(2))
                pool.wait_ge(root_made, a.pair + 1)
                gate(pool)
                c.wait()
                c.inc(G.tensor_tensor(by_tile(pair_h[:, :]), tiles_of(x3, a.t, 2),
                                      mean.unsqueeze(2).to_broadcast(wide), ALU.subtract))
                c.inc(G.tensor_scalar(v, var, EPS, None, ALU.add))
                c(G.tensor_tensor(z, root, root, ALU.mult))
                c(G.tensor_tensor(z, z, v, ALU.mult))
                c(G.tensor_scalar(z, z, -0.5, 1.5, ALU.mult, ALU.add))
                c(G.tensor_tensor(z, z, root, ALU.mult))
                c(G.tensor_tensor(by_tile(pair_h[:, :]), by_tile(pair_h[:, :]),
                                  z.unsqueeze(2).to_broadcast(wide), ALU.mult))
                c(G.tensor_scalar(pair_h[:, :], pair_h[:, :], 0.0, None, ALU.max))
                G.tensor_copy(table3[:, bass.ds(a.t, 2), 0:D], by_tile(pair_h[:, :])).then_inc(h_made, 1)
                c(G.tensor_tensor(h_sum[:, :], h_sum[:, :], pair_h[:, :], ALU.add))

            def step(w):
                if w.back(1):
                    reach_of(w.back(1))
                cur = w.back(2)
                if cur:
                    pool.wait_ge(indexed, cur.t + 1)
                    gather(layers[0], cur)
                if w.s % 2 == 0 and w.back(8):
                    residual(w.back(8))
                if w.s % 2 == 0 and w.back(6):
                    sums(w.back(6))
                if w.s % 2 and w.back(11):
                    normal(w.back(11))

            def step2(w):
                if w.back(0):
                    gather(layers[1], w.back(0))

            make_consts()
            pool.wait_ge(first_table.stored, 32)
            each_step(pool, NT, 12, step)
            pool.wait_ge(flag_made, 1)
            dense = pool.value_load(flag[0:1, 0:1], min_val=0, max_val=1)
            with pool.If(dense < 1):
                pool.wait_ge(pair_out, NT // 2 * 16)
                each_step(pool, NT, RING, step2)

        @block.scalar
        def _(act):
            A = nc.scalar

            def roots(B, k, n):
                at = slice(k * (NT // n), (k + 1) * (NT // n))
                act.wait_ge(B.var, k + 1)
                A.activation(stat[:, NT:2 * NT][:, at], stat[:, 0:NT][:, at], ACT.Ln, bias=eps[:, :]
                             ).then_inc(B.act, 1)
                act.wait_ge(B.act, k + 1)
                A.activation(stat[:, 2 * NT:3 * NT][:, at], stat[:, NT:2 * NT][:, at], ACT.Exp, scale=-0.5
                             ).then_inc(B.root, 1)

            def turn_weights(B):
                act.wait_ge(B.wT_ps, 1)
                A.copy(wT[:, :], sum_ps[0:D, 0:D]).then_inc(B.wT, 1)
                act.wait_ge(B.wa_ps, 1)
                A.copy(w_sb[:, D:R], sum_ps[0:D, 64:66]).then_inc(B.wa, 1)

            def make_table(B, quads):
                for q in quads:
                    act.wait_ge(B.hT_ps, q + 1)
                    if q >= 2:
                        act.wait_ge(B.rows_ps, q - 1)
                    A.copy(hT[q % 2][:, :], hT_ps[q % 2][0:D, :]).then_inc(B.hT, 1)
                    act.wait_ge(B.rows_ps, q + 1)
                    four = slice(4 * q, 4 * q + 4)
                    if B.layer == 0:
                        A.copy(table3[:, four, :], by_tile(rows_ps[q % 2][:, 0:4 * R], R)).then_inc(B.rows, 1)
                    else:
                        A.copy(table3[:, four, D:R], by_tile(rows_ps[q % 2][:, 0:8], 2)).then_inc(B.rows, 1)

            def mean(B):
                act.wait_ge(B.mean_ps, 1)
                A.copy(mean_row[B.layer][:, :], sum_ps[:, 0:D]).then_inc(B.mean, 1)

            def cast(cur, h):
                if h == 0:
                    act.wait_ge(adj_in[cur.par], cur.pair * 16 + 16)
                    if cur.static >= 2:
                        act.wait_ge(counted, cur.t - 1)
                if cur.static >= 1:
                    act.wait_ge(packs, cur.t * 2 - 1 + h)
                gate(act)
                A.activation(signs[h][:, :], adj[cur.par][:, h * HALF:(h + 1) * HALF], ACT.Sign,
                             accum_out=degree[cur.par][:, h:h + 1]).then_inc(casts, 1)

            def probs(L, t):
                act.wait_ge(L.shifted, t.t + 1)
                if t.static >= RING:
                    if L.n == 0:
                        act.wait_ge(recs, t.pair - 1)
                    else:
                        act.wait_ge(out_pairs, t.pair - 1)
                gate(act)
                sc = scores_of(t)
                A.activation(sc, sc, ACT.Exp, bias=shift[t.par][:, :],
                             accum_out=den[:, t.ring:t.ring + 1]).then_inc(L.probs, 1)

            def copy_s2(L, t, k):
                n = t.segments[k][3]
                act.wait_ge(L.s2T_turned, t.segment + (k + 1))
                A.copy(s2T[0:n, :], s2T_ps[0:n, 0:P]).then_inc(L.s2T_made, 1)

            def slopes(L, t, k):
                u, c0, e0, n = t.segments[k]
                g, w = t.segment + k, n * P
                if t.static or k:
                    act.wait_ge(L.masked, g)
                act.wait_ge(L.s2_spread, g + 1)
                gate(act)
                A.activation(slope[:, 0:w], s2_ps[:, 0:w], ACT.Identity, bias=col(s1_slope[L.n], t.t),
                             scale=ALPHA).then_inc(L.slope_made, 1)
                A.activation(mask[:, 0:w], edge_no[:, KMAX + e0:KMAX + e0 + w], ACT.Abs,
                             bias=col(middle, t.unit + u)).then_inc(L.distance_made, 1)

            def copy_turned(L, t):
                for k in range(t.groups):
                    chunks, buffer = place_of_group(t, k)
                    n = len(chunks) * P
                    act.wait_ge(L.turned, t.group + (k + 1))
                    if t.group_static + k >= 2:
                        act.wait_ge(L.group_summed, t.group + k - 1)
                    gate(act)
                    A.copy(buffer[:, 0:n], turned_ps[:, 0:n]).then_inc(L.turned_copied, 1)

            def step(w):
                L = layers[0]
                cur, t3, t4 = w.back(0), w.back(3), w.back(4)
                if cur and w.s:
                    cast(cur, 0)
                    cast(cur, 1)
                if t3:
                    act.wait_ge(pool_m, t3.t * 4 + 4)
                    gate(act)
                    for k in range(len(t3.segments)):
                        copy_s2(L, t3, k)
                        slopes(L, t3, k)
                if t4:
                    probs(L, t4)
                    copy_turned(L, t4)
                if w.s % 2 == 0 and w.back(8):
                    a = w.back(8)
                    act.wait_ge(neg_made, a.pair + 1)
                    A.activation(pair_b[:, :], pair_b[:, :], ACT.Exp).then_inc(exp_made, 1)
                if w.s % 2 and w.back(11):
                    a = w.back(11)
                    root = root2[a.ring // 2][:, :]
                    act.wait_ge(var_made, a.pair + 1)
                    if a.static >= 4:
                        act.wait_ge(pool_3, a.pair * 9 - 9)
                    gate(act)
                    A.activation(root, aggr[a.ring // 2][:, :].rearrange("p (t v) -> p t v", v=2)[:, :, 1],
                                 ACT.Ln, bias=eps[:, :]).then_inc(act_r, 1)
                    act.wait_ge(act_r, a.pair + 1)
                    A.activation(root, root, ACT.Exp, scale=-0.5).then_inc(root_made, 1)

            def step2(w):
                L = layers[1]
                cur, t1 = w.back(0), w.back(1)
                if cur:
                    copy_s2(L, cur, 0)
                if t1:
                    probs(L, t1)
                if cur:
                    slopes(L, cur, 0)
                    for k in range(1, len(cur.segments)):
                        copy_s2(L, cur, k)
                        slopes(L, cur, k)
                if t1:
                    copy_turned(L, t1)

            def dense_attend(L):
                with act.Fori(0, NT) as i:
                    act.wait_ge(L.shifted, i + 1)
                    gate(act)
                    A.activation(dense_scores, dense_scores, ACT.Exp, bias=shift[0][:, :],
                                 accum_out=den[:, 0:1]).then_inc(L.probs, 1)

            act.preload_act_table_set("natural_log_exp_and_others")
            B = first_table
            act.wait_ge(dve_c, 1)
            for k in range(PIECES // 2):
                roots(B, k, PIECES)
            turn_weights(B)
            make_table(B, range(0, NT // 8))
            first = Window(0, 0, NT).back(0)
            cast(first, 0)
            cast(first, 1)
            for k in range(PIECES // 2, PIECES):
                roots(B, k, PIECES)
            make_table(B, range(NT // 8, NT // 4))
            mean(B)
            A.mul(s1_slope[0][:, :], table3[:, :, D + 1], ALPHA).then_inc(s1_made, 1)
            A.copy(s1[0][:, :], table3[:, :, D + 1]).then_inc(s1_made, 1)
            act.wait_ge(s1_made, 2)
            each_step(act, NT, 12, step)
            act.wait_ge(flag_made, 1)
            dense = act.value_load(flag[0:1, 0:1], min_val=0, max_val=1)
            with act.If(dense < 1):
                act.wait_ge(row_made, NT // 2)
                A.mul(s1_slope[1][:, :], s1[1][:, :], ALPHA).then_inc(s1_made, 1)
                act.wait_ge(h_mean, 1)
                A.copy(mean_row[1][:, :], sum_ps[:, 0:D]).then_inc(h_total, 1)
                act.wait_ge(s1_made, 3)
                each_step(act, NT, 1, step2)
            with act.If(dense > 0):
                for L, B in zip(dense_layers, dense_tables):
                    roots(B, 0, 1)
                    if L.n == 0:
                        turn_weights(B)
                    make_table(B, range(NT // 4))
                    mean(B)
                    dense_attend(L)
                    if L.n == 0:
                        act.wait_ge(L.neg, 1)
                        A.activation(exp_b, exp_b, ACT.Exp).then_inc(L.exp, 1)

        @block.vector
        def _(dve):
            V = nc.vector

            def make_consts():
                c = Steps(dve, dve_c)
                c.inc(V.memset(eps[:, :], EPS))
                c.inc(V.memset(mean_of[:, :], 1.0 / N))
                at = 0
                for t in range(HEAD):
                    for _, chunks in units_of(t):
                        c.inc(V.memset(room[:, at:at + 1], float(chunks * P)))
                        at += 1
                c.inc(V.memset(room[:, at:NU], float(TAIL_UNITS[0][1] * P)))
                dve.wait_ge(consts, 9)
                c.inc(V.tensor_copy(select[:, :].rearrange("k (c p) -> k c p", p=P),
                                    identity[0:SEG, 0:SEG].unsqueeze(2).to_broadcast((SEG, SEG, P))))
                for b in range(BITS):
                    c.inc(V.tensor_scalar(weights[:, b * P:(b + 1) * P], identity[:, :], float(1 << b),
                                          None, ALU.mult))
                c.wait()
                return c.n

            def normalise(B, k, n, src3, centred3, square3, out3):
                at, m = slice(k * (NT // n), (k + 1) * (NT // n)), NT // n
                c = Steps(dve, B.step, 12 * k)
                var, _, y, z, mean = (stat[:, j * NT:(j + 1) * NT][:, at] for j in range(5))
                wide = (P, m, D)
                src, centred, square, out = (a[:, at, :] for a in (src3, centred3, square3, out3))
                c(V.tensor_reduce(mean, src, AX.X, ALU.add))
                c(V.tensor_scalar(mean, mean, 1.0 / D, None, ALU.mult))
                c(V.tensor_tensor(centred, src, mean.unsqueeze(2).to_broadcast(wide), ALU.subtract))
                c(V.tensor_tensor(square, centred, centred, ALU.mult))
                c(V.tensor_reduce(var, square, AX.X, ALU.add))
                V.tensor_scalar(var, var, 1.0 / D, None, ALU.mult).then_inc(B.var, 1)
                dve.wait_ge(B.var, k + 1)
                c(V.tensor_scalar(mean, var, EPS, None, ALU.add))
                dve.wait_ge(B.root, k + 1)
                c(V.tensor_tensor(z, y, y, ALU.mult))
                c(V.tensor_tensor(z, z, mean, ALU.mult))
                c(V.tensor_scalar(z, z, -0.5, 1.5, ALU.mult, ALU.add))
                c(V.tensor_tensor(z, y, z, ALU.mult))
                c(V.tensor_tensor(centred, centred, z.unsqueeze(2).to_broadcast(wide), ALU.mult))
                c(V.tensor_scalar(out, centred, 0.0, None, ALU.max))
                assert c.n == 12
                dve.sem_inc(B.h, 1)

            def take(cur):
                c = Steps(dve, dve_t, cur.take_step)
                rounds = word_rounds_of(cur.static)
                n, levels = 8 * rounds, cur.levels
                dve.wait_ge(packs, cur.t * 2 + 2)
                c(V.scalar_tensor_tensor(out=keys[:, :], in0=packed[cur.par][:, :], scalar=float(WORDS),
                                         in1=word_no[:, :], op0=ALU.mult, op1=ALU.add))
                src = keys
                for r in range(rounds):
                    best = found[:, 8 * r:8 * r + 8]
                    gate(dve)
                    c(V.max(best, src[:, :]))
                    if r < rounds - 1:
                        gate(dve)
                        dst = kept if src is keys else keys
                        c(V.match_replace(dst[:, :], best, src[:, :], USED))
                        src = dst
                f_i = found_i[:, 0:n]
                c(V.tensor_copy(f_i, found[:, 0:n]))
                c(V.tensor_scalar(f_i, f_i, OFFSET, 2 * OFFSET - 1, ALU.bitwise_xor, ALU.bitwise_and))
                c.inc(V.tensor_scalar(word_of[:, 0:n], f_i, WORDS - 1, None, ALU.bitwise_and))
                c(V.tensor_scalar(bits_i[:, 0:n], f_i, WORDS.bit_length() - 1, None,
                                  ALU.logical_shift_right))
                c(V.tensor_copy(bits[:, 0:n], bits_i[:, 0:n]))
                b_i = bits[:, 0:n].bitcast(I32)
                for level in range(levels):
                    if cur.static == 0:
                        out = ranked[:, 0:n] if level == 0 else lower[:, (level - 1) * n:level * n]
                    else:
                        out = lower[:, level * n:(level + 1) * n]
                    c.inc(V.scalar_tensor_tensor(out=out.bitcast(I32), in0=b_i, scalar=EXPONENT,
                                                 in1=word_of[:, 0:n], op0=ALU.bitwise_and,
                                                 op1=ALU.bitwise_or))
                    if level < levels - 1:
                        c(V.tensor_scalar(top_bit[:, 0:n].bitcast(I32), b_i, EXPONENT, None,
                                          ALU.bitwise_and))
                        c(V.tensor_tensor(bits[:, 0:n], bits[:, 0:n], top_bit[:, 0:n], ALU.subtract))
                c.wait()
                m = (levels - (cur.static == 0)) * n
                c(V.tensor_scalar(lower[:, 0:m], lower[:, 0:m], 0.25, None, ALU.max))
                last_rounds = cur.units[-1][0]
                at = n if cur.static == 0 else 0
                for r in range(last_rounds):
                    best = ranked[:, at + 8 * r:at + 8 * r + 8]
                    gate(dve)
                    c(V.max(best, lower[:, 0:m]))
                    if r < last_rounds - 1:
                        gate(dve)
                        c(V.match_replace(lower[:, 0:m], best, lower[:, 0:m], 0.25))
                n = cur.slots
                pairs = values[cur.par][:, 0:2 * n].rearrange("p (k v) -> p k v", v=2)
                r_i = ranked[:, 0:n].bitcast(I32)
                c.inc(V.tensor_scalar(exponent[:, 0:n], r_i, 23 - (WORDS.bit_length() - 1), ((1 << 9) - 1) * WORDS,
                                      ALU.logical_shift_right, ALU.bitwise_and))
                c(V.tensor_scalar(column[:, 0:n], r_i, WORDS - 1, None, ALU.bitwise_and))
                if cur.static >= 2:
                    dve.wait_ge(edged, cur.unit - len(units_of(cur.static - 1)))
                c(V.tensor_scalar(pairs[:, :, 1], exponent[:, 0:n], 126.0 * WORDS, 0.0, ALU.subtract, ALU.max))
                k, nu = 0, len(cur.units)
                for u, (r, _) in enumerate(cur.units):
                    c.inc(V.tensor_scalar(valid[:, k:k + 8 * r], pairs[:, k:k + 8 * r, 1], 0.5, None,
                                          ALU.is_ge, ALU.add, accum_out=col(count_all, cur.unit + u)))
                    k += 8 * r
                c.wait()
                c.inc(V.tensor_tensor(pairs[:, :, 0], column[:, 0:n], valid[:, 0:n], ALU.mult))
                found_n = col(count_all, cur.unit)
                if nu > 1:
                    found_n = total[:, 0:1]
                    c(V.tensor_reduce(found_n, col(count_all, cur.unit, nu), AX.X, ALU.add))
                d = degree[cur.par]
                V.scalar_tensor_tensor(out=col(missed, cur.t), in0=d[:, 0:1], scalar=d[:, 1:2],
                                       in1=found_n, op0=ALU.add, op1=ALU.subtract).then_inc(counted, 1)
                assert c.n == take_steps(cur.static), (cur.static, c.n, take_steps(cur.static))

            def index_of(t):
                dve.wait_ge(edged, t.unit + len(t.units))
                if t.static:
                    dve.wait_ge(indexed, t.t)
                n = t.chunks
                e = edges_ps[:, 0:2 * n].rearrange("p (c v) -> p c v", v=2)
                V.tensor_reduce(edge_f[:, 0:n], e, AX.X, ALU.add).then_inc(dve_i, 1)
                dve.wait_ge(dve_i, t.t + 1)
                V.tensor_scalar(col(index_all, t.chunk, n), edge_f[:, 0:n], float(-WORDS), 0.0, ALU.add,
                                ALU.max).then_inc(indexed, 1)

            def place_of(cur):
                nu = len(cur.units)
                dve.wait_ge(summed, cur.t + 1)
                V.tensor_copy(col(first_all, cur.unit, nu), starts_ps[:, 0:nu]).then_inc(firsts, 1)
                dve.wait_ge(firsts, cur.t + 1)
                for u, (r, chunks) in enumerate(cur.units):
                    if cur.static or u:
                        dve.wait_ge(edged, cur.unit + u)
                    V.tensor_scalar(place[:, 0:8 * r + chunks * P],
                                    edge_no[:, KMAX - 8 * r:KMAX + chunks * P],
                                    col(first_all, cur.unit + u), None, ALU.is_equal).then_inc(placed, 1)

            def score(L, cur):
                c = Steps(dve, L.dve, cur.score_step)
                sc = scores_of(cur)
                for k, (u, c0, e0, n) in enumerate(cur.segments):
                    g, w = cur.segment + k, n * P
                    dve.wait_ge(L.slope_made, g + 1)
                    V.scalar_tensor_tensor(out=leaky[:, 0:w], in0=s2_ps[:, 0:w], scalar=col(s1[L.n], cur.t),
                                           in1=slope[:, 0:w], op0=ALU.add, op1=ALU.max
                                           ).then_inc(L.s2_read, 1)
                    dve.wait_ge(L.distance_made, g + 1)
                    c.inc(V.tensor_scalar(mask[:, 0:w], mask[:, 0:w], col(reach, cur.unit + u), MASKED,
                                          ALU.is_gt, ALU.mult))
                    if k == 0 and cur.static >= 2:
                        dve.wait_ge(L.turned, cur.groups_until(2))
                    dve.wait_ge(L.s2_read, g + 1)
                    c.wait()
                    gate(dve)
                    V.tensor_tensor_reduce(
                        out=sc[:, c0 * P:c0 * P + w], in0=leaky[:, 0:w], in1=mask[:, 0:w], scale=1.0,
                        scalar=FLOOR, op0=ALU.add, op1=ALU.max, accum_out=top[:, k:k + 1]
                    ).then_inc(L.masked, 1)
                    dve.wait_ge(L.masked, g + 1)
                m = top[:, 0:1]
                if len(cur.segments) > 1:
                    m = top[:, 7:8]
                    c(V.tensor_reduce(m, top[:, 0:len(cur.segments)], AX.X, ALU.max))
                if cur.static >= 2:
                    dve.wait_ge(L.probs, cur.t - 1)
                V.tensor_scalar(shift[cur.par][:, :], m, -1.0, None, ALU.mult).then_inc(L.shifted, 1)
                dve.wait_ge(L.shifted, cur.t + 1)
                assert c.n == score_steps(cur.static) - 0, (cur.static, c.n)

            def copy_sum(L, t):
                dve.wait_ge(L.group_summed, t.group + t.groups)
                if L.n == 0 and t.static >= RING:
                    dve.wait_ge(neg_made, t.pair - 1)
                V.tensor_copy(acc3[:, t.ring:t.ring + 1, :], sum_ps[:, 0:D].unsqueeze(1)
                              ).then_inc(L.copied, 1)

            def reciprocals(a, s, pairs_done):
                d = den[:, a.ring:a.ring + 2]
                c = Steps(dve, s, pairs_done * 2)
                c(V.tensor_scalar(no_edge[:, :], d, 0.5, None, ALU.is_lt))
                c(V.tensor_tensor(rec[:, :], d, no_edge[:, :], ALU.add))

            def variance(a):
                dve.wait_ge(x1_made, a.pair + 1)
                if a.static >= 4:
                    dve.wait_ge(pool_3, a.pair * 9 - 9)
                for k in range(2):
                    V.bn_stats(stats[:, 6 * k:6 * k + 6], x3[:, bass.ds(a.t + k, 1), :]).then_inc(dve_v, 1)
                dve.wait_ge(dve_v, a.pair * 3 + 2)
                gate(dve)
                V.bn_aggr(aggr[a.ring // 2][:, 0:2], stats[:, 0:6]).then_inc(dve_v, 1)
                V.bn_aggr(aggr[a.ring // 2][:, 2:4], stats[:, 6:12]).then_inc(var_made, 1)
                dve.wait_ge(var_made, a.pair + 1)

            def dot(a):
                dve.wait_ge(h_made, a.pair + 1)
                for k in range(2):
                    for j, out in enumerate((s1[1][:, bass.ds(a.t + k, 1)],
                                             table3[:, bass.ds(a.t + k, 1), D])):
                        ins = V.scalar_tensor_tensor(
                            out=dots[:, :].unsqueeze(1), in0=table3[:, bass.ds(a.t + k, 1), 0:D], scalar=1.0,
                            in1=a_row[:, j * D:(j + 1) * D].unsqueeze(1), op0=ALU.mult, op1=ALU.mult,
                            accum_out=out)
                        if (k, j) == (1, 1):
                            ins.then_inc(row_made, 1)
                            dve.wait_ge(row_made, a.pair + 1)
                        else:
                            ins.then_inc(dve_d, 1)
                            dve.wait_ge(dve_d, a.pair * 3 + (2 * k + j + 1))

            def step(w):
                L = layers[0]
                if w.back(0):
                    take(w.back(0))
                if w.back(3):
                    score(L, w.back(3))
                if w.back(1):
                    index_of(w.back(1))
                if w.back(4):
                    copy_sum(L, w.back(4))
                if w.s % 2 and w.back(5):
                    a = w.back(5)
                    if a.static >= 2:
                        dve.wait_ge(neg_made, a.pair)
                    reciprocals(a, dve_r, a.pair)
                    V.reciprocal(rec[:, :], rec[:, :]).then_inc(recs, 1)
                if w.s % 2 and w.back(9):
                    variance(w.back(9))
                if w.s % 2 == 0 and w.back(12):
                    dot(w.back(12))
                if w.back(0):
                    place_of(w.back(0))

            def judge():
                c = Steps(dve, dve_f)
                dve.wait_ge(counted, NT)
                dve.wait_ge(firsts, NT)
                c.inc(V.tensor_reduce(fault[:, 0:1], missed[:, :], AX.X, ALU.max,
                                      apply_absolute_value=True))
                c(V.tensor_tensor(half_count[:, :], first_all[:, :], count_all[:, :], ALU.add))
                c(V.tensor_tensor(half_count[:, :], half_count[:, :], room[:, :], ALU.subtract))
                c.inc(V.tensor_reduce(fault[:, 1:2], half_count[:, :], AX.X, ALU.max))
                c(V.memset(fault[:, 3:4], 1.0))
                V.tensor_scalar(fault[:, 2:3], fault[:, 0:1], fault[:, 1:2], 0.0, ALU.max, ALU.is_gt
                                ).then_inc(fault_made, 1)
                dve.wait_ge(fault_sum, 1)
                V.tensor_scalar(flag[0:1, 0:1], edges_ps[0:1, 256:257], 0.0, None, ALU.is_gt
                                ).then_inc(flag_made, 1)
                dve.wait_ge(flag_made, 1)

            out_step = sem("dve_out_step")

            def finish(a):
                wide = (P, 2, D)
                c = Steps(dve, out_step, a.pair * 6)
                c.wait() if a.static else None
                reciprocals(a, out_step, a.pair * 3)
                c.n = 2
                c(V.reciprocal(rec[:, :], rec[:, :]))
                c.inc(V.tensor_tensor(by_tile(pair_a[:, :]), acc3[:, a.ring:a.ring + 2, :],
                                      rec[:, :].unsqueeze(2).to_broadcast(wide), ALU.mult))
                c(V.tensor_tensor(by_tile(pair_b[:, :]), no_edge[:, :].unsqueeze(2).to_broadcast(wide),
                                  mean_row[1][:, :].unsqueeze(1).to_broadcast(wide), ALU.mult))
                c(V.tensor_tensor(pair_a[:, :], pair_a[:, :], pair_b[:, :], ALU.add))
                x = tiles_of(x3, a.t, 2)
                V.scalar_tensor_tensor(out=x, in0=by_tile(pair_a[:, :]), scalar=0.0, in1=x, op0=ALU.max,
                                       op1=ALU.add).then_inc(out_pairs, 1)
                dve.wait_ge(out_pairs, a.pair + 1)

            def step2(w):
                L = layers[1]
                if w.back(0):
                    score(L, w.back(0))
                if w.back(1):
                    copy_sum(L, w.back(1))
                if w.s % 2 == 0 and w.back(2):
                    dve.wait_ge(L.copied, w.back(2).t + 2)
                    finish(w.back(2))

            def dense_attend(L):
                BLK = SEG * P
                dve.wait_ge(L.s2, 48)
                per_tile = 1 + 3 * (N // BLK) + 1 + 2
                with dve.Fori(0, NT) as i:
                    c = Steps(dve, L.dve, i * per_tile)
                    dve.wait_ge(L.adj, i * 16 + 16)
                    c(V.tensor_scalar(dense_scores, adj[0][:, :], 0.0, MASKED, ALU.is_le, ALU.mult))
                    for k in range(N // BLK):
                        at = slice(k * BLK, (k + 1) * BLK)
                        c(V.tensor_scalar(slope[:, :], s2_row[:, at],
                                          table3[:, bass.ds(i, 1), D + 1], None, ALU.add))
                        c(V.scalar_tensor_tensor(out=leaky[:, :], in0=slope[:, :], scalar=ALPHA,
                                                 in1=slope[:, :], op0=ALU.mult, op1=ALU.max))
                        gate(dve)
                        c(V.tensor_tensor_reduce(
                            out=dense_scores[:, at], in0=leaky[:, :], in1=dense_scores[:, at],
                            scale=1.0, scalar=FLOOR, op0=ALU.add, op1=ALU.max,
                            accum_out=found[:, k:k + 1]))
                    c(V.tensor_reduce(top[:, 0:1], found[:, 0:N // BLK], AX.X, ALU.max))
                    V.tensor_scalar(shift[0][:, :], top[:, 0:1], -1.0, None, ALU.mult
                                    ).then_inc(L.shifted, 1)
                    for q in range(NT // 4):
                        dve.wait_ge(L.turned, i * (NT // 4) + (q + 1))
                        V.tensor_copy(probsT[0][:, :], turned_ps[:, :]).then_inc(L.copied, 1)
                    dve.wait_ge(L.summed, i + 1)
                    c.inc(V.tensor_copy(tiles_of(agg3, i), sum_ps[:, 0:D].unsqueeze(1)))
                    c.inc(V.tensor_copy(col(den_all, i), den[:, 0:1]))
                    c.wait()
                    dve.sem_inc(L.done, 1)
                    assert c.n == per_tile, c.n

            def dense_divide(L, c):
                none, r = stat[:, 0:NT], stat[:, NT:2 * NT]
                c(V.tensor_scalar(none, den_all[:, :], 0.5, None, ALU.is_lt))
                c(V.tensor_tensor(r, den_all[:, :], none, ALU.add))
                c(V.reciprocal(r, r))
                wide = (P, NT, D)
                c(V.tensor_tensor(agg3, agg3, r.unsqueeze(2).to_broadcast(wide), ALU.mult))
                c(V.tensor_tensor(by_tile(exp_b), none.unsqueeze(2).to_broadcast(wide),
                                  mean_row[L.n][:, :].unsqueeze(1).to_broadcast(wide), ALU.mult))
                c(V.tensor_tensor(agg[:, :], agg[:, :], exp_b, ALU.add))

            make_consts()
            dve.wait_ge(x_in, 32)
            for k in range(PIECES):
                normalise(first_table, k, PIECES, x3, agg3, table3[:, :, 0:D], agg3)
            dve.wait_ge(s1_made, 2)
            each_step(dve, NT, 12, step)
            judge()
            dense = dve.value_load(flag[0:1, 0:1], min_val=0, max_val=1)
            with dve.If(dense < 1):
                dve.wait_ge(h_total, 1)
                each_step(dve, NT, 2, step2)
            with dve.If(dense > 0):
                dve.wait_ge(x_again, 32)
                normalise(dense_tables[0], 0, 1, x3, by_tile(centred_b), by_tile(square_b), agg3)
                for L, B in zip(dense_layers, dense_tables):
                    dve.wait_ge(B.mean, 1)
                    dense_attend(L)
                    c = Steps(dve, L.post)
                    dense_divide(L, c)
                    if L.n == 0:
                        dve.wait_ge(L.x_in, 32)
                        V.tensor_scalar(exp_b, agg[:, :], 0.0, None, ALU.min).then_inc(L.neg, 1)
                        dve.wait_ge(L.exp, 1)
                        c(V.scalar_tensor_tensor(out=agg[:, :], in0=exp_b, scalar=-1.0, in1=agg[:, :],
                                                 op0=ALU.add, op1=ALU.max))
                        c(V.tensor_tensor(agg[:, :], agg[:, :], x_b, ALU.add))
                        dve.sem_inc(L.x_out, 1)
                        normalise(dense_tables[1], 0, 1, agg3, by_tile(centred_b), by_tile(square_b),
                                  table3[:, :, 0:D])
                        dve.wait_ge(L.x_in, 48)
                    else:
                        dve.wait_ge(L.x_in, 16)
                        V.scalar_tensor_tensor(out=agg[:, :], in0=agg[:, :], scalar=0.0, in1=x_b,
                                               op0=ALU.max, op1=ALU.add).then_inc(L.x_out, 1)

        @block.tensor
        def _(pe):
            T = nc.tensor

            def turn_weights(B):
                T.transpose(sum_ps[0:D, 0:D], w_sb[:, 0:D], identity[0:D, 0:D]).then_inc(B.wT_ps, 1)
                pe.wait_ge(B.wT, 1)
                T.matmul(sum_ps[0:D, 64:66], wT[:, :], a_sb[:, 0:2], start=True, stop=True
                         ).then_inc(B.wa_ps, 1)
                pe.wait_ge(B.wa, 1)

            def make_table(B, quads, pieces):
                rhs, n = (w_sb[:, :], R) if B.layer == 0 else (a_sb[:, 2:4], 2)
                for q in quads:
                    pe.wait_ge(B.h, q * pieces // (NT // 4) + 1)
                    if q >= 2:
                        pe.wait_ge(B.hT, q - 1)
                    for k in range(4):
                        t = 4 * q + k
                        h = agg3[:, t, :] if B.layer == 0 else table3[:, t, 0:D]
                        last = T.transpose(hT_ps[q % 2][0:D, k * P:(k + 1) * P], h, identity[:, :])
                    last.then_inc(B.hT_ps, 1)
                    pe.wait_ge(B.hT, q + 1)
                    if q >= 2:
                        pe.wait_ge(B.rows, q - 1)
                    for k in range(4):
                        last = T.matmul(rows_ps[q % 2][:, n * k:n * k + n], hT[q % 2][:, k * P:(k + 1) * P],
                                        rhs, start=True, stop=True)
                    last.then_inc(B.rows_ps, 1)

            def mean(B):
                pe.wait_ge(B.rows, NT // 4)
                for t in range(NT):
                    last = T.matmul(sum_ps[:, 0:D], mean_of[:, :], table3[:, t, 0:D], start=(t == 0),
                                    stop=(t == NT - 1))
                last.then_inc(B.mean_ps, 1)

            def words_of(cur, h):
                pe.wait_ge(casts, cur.t * 2 + (h + 1))
                if h == 0 and cur.static >= 2:
                    pe.wait_ge(counted, cur.t - 1)
                for b in range(BITS // 2):
                    bit = h * (BITS // 2) + b
                    last = T.matmul(packed[cur.par][:, :], weights[:, bit * P:(bit + 1) * P],
                                    signs[h][:, b * WORDS:(b + 1) * WORDS], start=(bit == 0),
                                    stop=(bit == BITS - 1))
                last.then_inc(packs, 1)

            def starts(t):
                pe.wait_ge(counted, t.t + 1)
                nu = len(t.units)
                T.matmul(starts_ps[:, 0:nu], before[:, :], col(count_all, t.unit, nu), start=True,
                         stop=True).then_inc(summed, 1)

            def pack_edges(t):
                slot, chunk = 0, 0
                for u, (r, chunks) in enumerate(t.units):
                    pe.wait_ge(placed, t.unit + (u + 1))
                    for c in range(chunks):
                        at = 2 * (chunk + c)
                        for k in range(8 * r):
                            src = 8 * r - k + c * P
                            last = T.matmul(edges_ps[:, at:at + 2], place[:, src:src + P],
                                            values[t.par][:, 2 * (slot + k):2 * (slot + k) + 2],
                                            start=(k == 0), stop=(k == 8 * r - 1))
                    last.then_inc(edged, 1)
                    slot += 8 * r
                    chunk += chunks

            def turn_s2(L, t, k):
                u, c0, e0, n = t.segments[k]
                if k == 0:
                    pe.wait_ge(L.rows_in[t.ring], (t.ring_chunks + t.chunks) * 16)
                if t.static or k:
                    pe.wait_ge(L.s2T_made, t.segment + k)
                s2 = by_tile(rows[t.ring][:, c0 * RG:(c0 + n) * RG], RG)[:, :, D]
                T.transpose(s2T_ps[0:n, 0:P], s2, identity[:, :]).then_inc(L.s2T_turned, 1)

            def spread_s2(L, t, k):
                n = t.segments[k][3]
                pe.wait_ge(L.s2T_made, t.segment + (k + 1))
                if t.static or k:
                    pe.wait_ge(L.s2_read, t.segment + k)
                for c in range(n):
                    last = T.matmul(s2_ps[:, c * P:(c + 1) * P], select[0:n, c * P:(c + 1) * P],
                                    s2T[0:n, :], start=True, stop=True)
                last.then_inc(L.s2_spread, 1)

            def turn_probs(L, t, k):
                if k == 0:
                    pe.wait_ge(L.probs, t.t + 1)
                if t.static or k:
                    pe.wait_ge(L.turned_copied, t.group + k)
                chunks, _ = place_of_group(t, k)
                sc = scores_of(t)
                for c in chunks:
                    last = T.transpose(turned_ps[:, (c % 4) * P:(c % 4 + 1) * P],
                                       sc[:, c * P:(c + 1) * P], identity[:, :])
                last.then_inc(L.turned, 1)

            def sum_rows(L, t):
                for k in range(t.groups):
                    if k:
                        turn_probs(L, t, k)
                    chunks, buffer = place_of_group(t, k)
                    pe.wait_ge(L.turned_copied, t.group + (k + 1))
                    if k == 0 and t.static:
                        pe.wait_ge(L.copied, t.t)
                    for c in chunks:
                        last = T.matmul(sum_ps[:, 0:D], buffer[:, (c % 4) * P:(c % 4 + 1) * P],
                                        rows[t.ring][:, c * RG:c * RG + D], start=(c == 0),
                                        stop=(c == t.chunks - 1))
                    last.then_inc(L.group_summed, 1)

            def step(w):
                L = layers[0]
                cur, t1, t3, t4 = (w.back(k) for k in (0, 1, 3, 4))
                if cur and w.s:
                    words_of(cur, 0)
                    words_of(cur, 1)
                if t3:
                    turn_s2(L, t3, 0)
                    spread_s2(L, t3, 0)
                if t1:
                    starts(t1)
                    pack_edges(t1)
                if t3:
                    for k in range(1, len(t3.segments)):
                        turn_s2(L, t3, k)
                        spread_s2(L, t3, k)
                if t4:
                    turn_probs(L, t4, 0)
                    sum_rows(L, t4)

            def step2(w):
                L = layers[1]
                cur, t1 = w.back(0), w.back(1)
                if cur:
                    turn_s2(L, cur, 0)
                    spread_s2(L, cur, 0)
                if t1:
                    turn_probs(L, t1, 0)
                if cur:
                    for k in range(1, len(cur.segments)):
                        turn_s2(L, cur, k)
                        spread_s2(L, cur, k)
                if t1:
                    sum_rows(L, t1)

            def chunk_of(sc, c):
                if c < HEAD:
                    return sc[:, c * P:(c + 1) * P]
                return sc[:, HEAD * P:N].rearrange("p (k t) -> p t k", t=TAIL)[:, c - HEAD, :]

            def dense_attend(L):
                with pe.Fori(0, NT) as i:
                    pe.wait_ge(L.probs, i + 1)
                    for q in range(NT // 4):
                        for k in range(4):
                            last = T.transpose(turned_ps[:, k * P:(k + 1) * P],
                                               chunk_of(dense_scores, 4 * q + k), identity[:, :])
                        last.then_inc(L.turned, 1)
                        pe.wait_ge(L.copied, i * (NT // 4) + (q + 1))
                        for k in range(4):
                            c = 4 * q + k
                            last = T.matmul(sum_ps[:, 0:D], probsT[0][:, k * P:(k + 1) * P],
                                            table3[:, c, 0:D], start=(c == 0), stop=(c == NT - 1))
                    last.then_inc(L.summed, 1)

            B = first_table
            pe.wait_ge(consts, 9)
            pe.wait_ge(w_in, 6 * 16)
            turn_weights(B)
            make_table(B, range(0, NT // 8), PIECES)
            first = Window(0, 0, NT).back(0)
            pe.wait_ge(dve_c, 3 + sum(len(units_of(t)) for t in range(HEAD)) + 1 + BITS)
            words_of(first, 0)
            words_of(first, 1)
            make_table(B, range(NT // 8, NT // 4), PIECES)
            mean(B)
            pe.wait_ge(B.mean, 1)
            each_step(pe, NT, 4, step)
            pe.wait_ge(fault_made, 1)
            T.matmul(edges_ps[0:1, 256:257], fault[:, 2:3], fault[:, 3:4], start=True, stop=True
                     ).then_inc(fault_sum, 1)
            pe.wait_ge(flag_made, 1)
            dense = pe.value_load(flag[0:1, 0:1], min_val=0, max_val=1)
            with pe.If(dense < 1):
                pe.wait_ge(pool_3, NT // 2 * 9)
                for k in range(2):
                    last = T.matmul(sum_ps[:, 0:D], mean_of[:, :], h_sum[:, k * D:(k + 1) * D],
                                    start=(k == 0), stop=(k == 1))
                last.then_inc(h_mean, 1)
                pe.wait_ge(h_total, 1)
                each_step(pe, NT, 1, step2)
            with pe.If(dense > 0):
                for L, B in zip(dense_layers, dense_tables):
                    if L.n == 0:
                        pe.wait_ge(B.h, 1)
                        turn_weights(B)
                    make_table(B, range(NT // 4), 1)
                    mean(B)
                    pe.wait_ge(B.mean, 1)
                    dense_attend(L)


_INS = ["x", "adj", "L0_gnn_W", "L0_gnn_a", "L1_gnn_a"]


def kernel(**inputs):
    import numpy as np
    import concourse.bacc as bacc
    from concourse.bass_utils import run_bass_kernel_spmd

    nc = bacc.Bacc("TRN2", target_bir_lowering=False, num_devices=1)
    arrays = {f"in_{name}": np.ascontiguousarray(inputs[name]) for name in _INS}
    aps = [nc.dram_tensor(name, a.shape, mybir.dt.from_np(a.dtype), kind="ExternalInput").ap()
           for name, a in arrays.items()]
    out = nc.dram_tensor("out", arrays["in_x"].shape, F32, kind="ExternalOutput").ap()
    gat_kernel(nc, *aps, out)
    return run_bass_kernel_spmd(nc, [arrays], core_ids=[0]).results[0]["out"]
```

```python
import concourse.bass as bass
from concourse import mybir
from contextlib import ExitStack

F32 = mybir.dt.float32
F16 = mybir.dt.float16
I32 = mybir.dt.int32
U32 = mybir.dt.uint32
I16 = mybir.dt.int16
ALU = mybir.AluOpType
ACT = mybir.ActivationFunctionType
AX = mybir.AxisListType

P = 128
ALPHA = 0.2
EPS = 1e-5
MASKED = -9.0e15
FLOOR = -1.0e15
BITS = 16
EXPONENT = 0x7F800000
OFFSET = 1 << 24
USED = -3.0e38
SEG = 4
ROWS = 8
RING = 4
UNROLL = ROWS

HEAD_UNITS = [
    [(2, 16), (2, 4), (4, 2), (8, 1), (3, 1)], [(3, 8)], [(3, 6)], [(3, 6)],
    [(2, 5)], [(2, 5)], [(2, 4)], [(2, 4)],
]
TAIL_UNITS = [(2, 2)]
HEAD = len(HEAD_UNITS)
LEVELS0, LEVELS_HEAD, LEVELS_TAIL = 5, 4, 3


def units_of(t):
    return HEAD_UNITS[t] if t < HEAD else TAIL_UNITS


def levels_of(t):
    return LEVELS0 if t == 0 else LEVELS_HEAD if t < HEAD else LEVELS_TAIL


def chunks_of(t):
    return sum(c for _, c in units_of(t))


def groups_of(t):
    return -(-chunks_of(t) // 4)


def segments_of(t):
    out, at = [], 0
    for u, (_, c) in enumerate(units_of(t)):
        for k in range(0, c, SEG):
            out.append((u, at + k, k * P, min(SEG, c - k)))
        at += c
    return out


def word_rounds_of(t):
    return sum(r for r, _ in (units_of(t)[:-1] if t == 0 else units_of(t)))


def take_steps(t):
    rounds, units, levels = word_rounds_of(t), len(units_of(t)), levels_of(t)
    best = 2 * units_of(t)[-1][0] - 1
    return 2 * rounds + 5 + 3 * levels - 2 + 1 + best + 4 + units + (units > 1)


def score_steps(t):
    return len(segments_of(t)) + (len(segments_of(t)) > 1)


class Tile:

    def __init__(self, t, i=0):
        def so_far(of, tiles=None, per_turn=UNROLL):
            return sum(of(k) for k in (range(t) if tiles is None else tiles)) + i * (per_turn * of(t))

        self.static, self.t = t, i * UNROLL + t
        self.par, self.ring, self.slot = t % 2, t % RING, t % ROWS
        self.pair = i * (UNROLL // 2) + t // 2
        self.units, self.chunks, self.groups = units_of(t), chunks_of(t), groups_of(t)
        self.segments, self.levels = segments_of(t), levels_of(t)
        self.slots = 8 * sum(r for r, _ in self.units)
        self.chunk = so_far(chunks_of)
        self.unit = so_far(lambda k: len(units_of(k)))
        self.segment = so_far(lambda k: len(segments_of(k)))
        self.group = so_far(groups_of)
        self.group_static = sum(groups_of(k) for k in range(t))
        self.segment_static = sum(len(segments_of(k)) for k in range(t))
        self.slot_chunks = so_far(chunks_of, range(t % ROWS, t, ROWS), 1)
        self.take_step = so_far(take_steps)
        self.score_step = so_far(score_steps)

    def groups_until(self, back):
        return self.group - sum(groups_of(k) for k in range(self.static - back + 1, self.static))


class Window:

    def __init__(self, s, i, tiles):
        self.s, self.i, self.tiles = s, i, tiles

    def back(self, k):
        return Tile(self.s - k, self.i) if 0 <= self.s - k < self.tiles else None


def each_step(eng, tiles, lag, step):
    first = -(-(HEAD + lag) // UNROLL) * UNROLL
    for s in range(first):
        step(Window(s, 0, tiles))
    with eng.Fori(0, (tiles - first) // UNROLL) as i:
        for s in range(first, first + UNROLL):
            step(Window(s, i, tiles))
    for s in range(tiles, tiles + lag):
        step(Window(s, 0, tiles))


def gat_kernel(nc, x_d, adj_d, w_d, a0_d, a1_d, out_d):
    N, D = x_d.shape
    NT = N // P
    WORDS = N // BITS
    HALF = N // 2
    TAIL = NT - HEAD
    NCH = sum(chunks_of(t) for t in range(NT))
    NU = sum(len(units_of(t)) for t in range(NT))
    C0 = chunks_of(0)
    KMAX = max(8 * r for t in range(NT) for r, _ in units_of(t))
    EMAX = P * max(c for t in range(NT) for _, c in units_of(t))
    SLOTS = Tile(0).slots
    BELOW = max((levels_of(0) - 1) * 8 * word_rounds_of(0),
                max(levels_of(t) * 8 * word_rounds_of(t) for t in range(1, NT)))
    R = D + 2
    RG = D + 1
    SZ = NT * D
    PIECES = 4

    table_d = [nc.dram_tensor(f"table{n}", (N, RG), F32, kind="Internal").ap() for n in range(2)]
    s2_d = [nc.dram_tensor(f"s2_{n}", (N, 1), F32, kind="Internal").ap() for n in range(2)]
    x1_d = nc.dram_tensor("x1_scratch", (P, SZ), F32, kind="Internal").ap()

    ctx = ExitStack()
    with ctx:
        def sb(name, shape, dt=F32):
            return ctx.enter_context(nc.sbuf_tensor(name, shape, dt))

        def sem(name):
            return ctx.enter_context(nc.semaphore(name))

        def chunks_in(part, parts, start):
            return max(chunks_of(t) for t in range(start, NT) if t % parts == part)

        def by_tile(ap, width=D):
            return ap.rearrange("p (t d) -> p t d", d=width)

        adj = [sb(f"adj{b}", [P, N], I32) for b in range(2)]
        signs = [sb(f"signs{b}", [P, HALF], F16) for b in range(2)]
        table = sb("table", [P, NT * R])
        table3 = by_tile(table[:, :], R)
        x_all = sb("x_all", [P, SZ])
        x3 = by_tile(x_all[:, :])
        agg = sb("agg", [P, SZ])
        agg3 = by_tile(agg[:, :])
        big_scores = agg[:, SZ - C0 * P:SZ]

        identity = sb("identity", [P, P])
        weights = sb("weights", [P, BITS * P], F16)
        before = sb("before", [P, P])
        halves, quarters = (sb(n, [P, len(HEAD_UNITS[0])]) for n in ("halves", "quarters"))
        word_no = sb("word_no", [P, WORDS])
        edge_no = sb("edge_no", [P, KMAX + EMAX], I16)
        ones = sb("ones", [P, P])
        room = sb("room", [P, NU])
        eps = sb("eps", [P, 1])

        keys = sb("keys", [P, WORDS])
        kept = sb("kept", [P, WORDS])
        found = sb("found", [P, 8 * word_rounds_of(0)])
        found_i = sb("found_i", [P, 8 * word_rounds_of(0)], I32)
        word_of = sb("word_of", [P, 8 * word_rounds_of(0)], I32)
        bits_i = sb("bits_i", [P, 8 * word_rounds_of(0)], I32)
        bits = sb("bits", [P, 8 * word_rounds_of(0)])
        top_bit = sb("top_bit", [P, 8 * word_rounds_of(0)])
        lower = sb("lower", [P, BELOW])
        ranked = sb("ranked", [P, SLOTS])
        exponent = sb("exponent", [P, SLOTS], I32)
        column = sb("column", [P, SLOTS], I32)
        valid = sb("valid", [P, SLOTS])
        values = [sb(f"values{b}", [P, 2 * SLOTS], F16) for b in range(2)]
        degree = [sb(f"degree{b}", [P, 2]) for b in range(2)]
        total = sb("total", [P, 1])
        place = sb("place", [P, KMAX + EMAX], F16)
        edge_f = sb("edge_f", [P, C0])
        missed = sb("missed", [P, NT])
        count_all = sb("count_all", [P, NU])
        first_all = sb("first_all", [P, NU])
        middle = sb("middle", [P, NU])
        half_count = sb("half_count", [P, NU])
        reach = sb("reach", [P, NU])
        index_all = sb("index_all", [P, NCH], U32)
        fault = sb("fault", [P, 4])
        flag = sb("flag", [1, 1], I32)

        index = [sb(f"index{r}", [P, chunks_in(r, ROWS, 0)], U32) for r in range(ROWS)]
        rows = [sb(f"rows{r}", [P, chunks_in(r, ROWS, 0) * RG]) for r in range(ROWS)]
        diagonal = sb("diagonal", [P, SEG * P])
        slopes_of = [sb("slope0", [P, SEG * P]), agg[:, 0:SEG * P]]
        masks_of = [sb("mask0", [P, SEG * P]), agg[:, SEG * P:2 * SEG * P]]
        leaky = sb("leaky", [P, SEG * P])
        scores = [sb(f"scores{r}", [P, chunks_in(r, RING, 1) * P]) for r in range(RING)]
        top = sb("top", [P, 8])
        shift = [sb(f"shift{b}", [P, 1]) for b in range(2)]
        den = sb("den", [P, RING])
        no_edge = sb("no_edge", [P, 2])
        rec = sb("rec", [P, 2])
        acc = sb("acc", [P, RING * D])
        acc3 = by_tile(acc[:, :])
        probsT = [sb(f"probsT{b}", [P, 512]) for b in range(2)]
        s1 = [sb(f"s1_{n}", [P, NT]) for n in range(2)]
        s1_slope = [sb(f"s1_slope{n}", [P, NT]) for n in range(2)]
        mean_row = [sb(f"mean_row{n}", [P, D]) for n in range(2)]

        pair_a, pair_b = sb("pair_a", [P, 2 * D]), sb("pair_b", [P, 2 * D])
        pair_s = [sb(f"pair_s{b}", [P, 4]) for b in range(2)]
        var_eps = sb("var_eps", [P, 2])
        root2 = [sb(f"root2_{b}", [P, 2]) for b in range(2)]
        stats = sb("stats", [P, 2 * 6])
        aggr = [sb(f"aggr{b}", [P, 4]) for b in range(2)]
        h_sum = sb("h_sum", [P, D])
        dots = sb("dots", [P, D])
        a_row = sb("a_row", [P, 2 * D])

        stat = sb("stat", [P, 5 * NT])
        den_all = sb("den_all", [P, NT])
        w_sb = sb("w_sb", [D, R])
        wT = sb("wT", [D, D])
        a_sb = sb("a_sb", [D, 4])
        hT = [probsT[b][0:D, :] for b in range(2)]

        bufs = [adj[b][:, k * SZ:(k + 1) * SZ].bitcast(F32) for b in range(2) for k in range(2)]
        x_b, exp_b, centred_b, square_b = bufs
        s2_row = adj[1][:, :].bitcast(F32)
        dense_scores = adj[0][:, :].bitcast(F32)

        def ps(name, shape):
            return ctx.enter_context(nc.psum_tensor(name, shape, F32))

        packed = [ps(f"packed{b}", [P, WORDS]) for b in range(2)]
        starts_ps, edges_ps = ps("starts_ps", [P, 512]), ps("edges_ps", [P, 512])
        s2_ps = [ps(f"s2_ps{b}", [P, 512]) for b in range(2)]
        turned_ps, sum_ps = ps("turned_ps", [P, 512]), ps("sum_ps", [P, 512])
        hT_ps = [turned_ps, s2_ps[1]]
        rows_ps = [s2_ps[0], sum_ps]

        consts, dve_c = sem("consts_made"), sem("dve_const_step")
        x_in, w_in, x_again = sem("x_in"), sem("w_in"), sem("x_again")
        adj_in = [sem(f"adj_in{b}") for b in range(2)]
        casts, packs, counted = sem("signs_made"), sem("halves_packed"), sem("edges_counted")
        summed, placed, edged = sem("starts_summed"), sem("places_made"), sem("edges_packed")
        indexed, firsts = sem("indices_made"), sem("firsts_copied")
        dve_t, dve_i, dve_f = sem("dve_take_step"), sem("dve_index_step"), sem("dve_fault_step")
        fault_made, fault_sum, flag_made = sem("fault_made"), sem("fault_summed"), sem("flag_made")
        gates = sem("gate")
        recs, neg_made, exp_made = sem("recs_made"), sem("neg_made"), sem("exp_made")
        x1_made, var_made, root_made, h_made = sem("x1_made"), sem("var_made"), sem("root_made"), sem("h_made")
        pair_out = sem("pair_rows_stored")
        pool_1, pool_2, h_summed = sem("pool_sum_step"), sem("pool_x_step"), sem("h_summed")
        dve_v, dots_made, act_r = sem("dve_var_step"), sem("dots_made"), sem("act_root_step")
        root_step = sem("dve_root_step")
        h_mean, h_total, s1_made, out_pairs, out_in = (sem("h_mean_summed"), sem("h_mean_made"), sem("s1_slope_made"),
                                                       sem("out_pairs_made"), sem("out_stored"))
        pool_m = sem("reach_made")

        class Table:

            def __init__(self, n, spare=None):
                def s(name):
                    return spare.signals.pop() if spare and spare.signals else sem(f"{name}_t{n}")
                self.n, self.layer = n, {0: 0, 2: 0, 3: 1}[n]
                self.step, self.act, self.var, self.root, self.h = (
                    s("dve_step"), s("act_step"), s("var_made"), s("root_made"), s("h_made"))
                self.wT_ps, self.wT, self.wa_ps, self.wa = s("wT_ps"), s("wT"), s("wa_ps"), s("wa")
                self.hT_ps, self.hT, self.rows_ps, self.rows = s("hT_ps"), s("hT"), s("rows_ps"), s("rows")
                self.centred, self.squared = s("centred"), s("squared")
                self.summed, self.mean_ps, self.mean, self.stored = s("summed"), s("mean_ps"), s("mean"), s("stored")

        class Attention:

            def __init__(self, n):
                def s(name):
                    self.signals.append(sem(f"{name}_{n}"))
                    return self.signals[-1]
                self.n, self.signals = n, []
                self.index_copied, self.rows_in = s("index_copied"), [s(f"rows_in{r}") for r in range(ROWS)]
                self.diagonal_made, self.s2_spread = s("diagonal_made"), s("s2_spread")
                self.slope_made, self.distance_made, self.s2_read = (
                    s("slope_made"), s("distance_made"), s("s2_read"))
                self.masked, self.dve, self.shifted, self.probs = (
                    s("masked"), s("dve_score_step"), s("shifted"), s("probs_made"))
                self.turned, self.turned_copied, self.group_summed = (
                    s("turned"), s("turned_copied"), s("group_summed"))
                self.copied = s("sums_copied")

        class Dense:

            def __init__(self, n, spare=None):
                def s(name):
                    return spare.signals.pop() if spare else sem(f"dense_{name}_{n}")
                self.n = n
                self.s2, self.adj, self.dve, self.shifted, self.probs = (
                    s("s2"), s("adj_in"), s("dve_step"), s("shifted"), s("probs"))
                self.turned, self.copied, self.summed, self.done = s("turned"), s("copied"), s("summed"), s("done")
                self.post, self.neg, self.exp, self.x_in, self.x_out = s("post"), s("neg"), s("exp"), s("x_in"), s("x_out")

        layers = [Attention(0), Attention(1)]
        dense_layers = [Dense(0, layers[1]), Dense(1)]
        first_table, dense_tables = Table(0), [Table(2, layers[1]), Table(3)]

        block = ctx.enter_context(nc.Block())

        class Steps:

            def __init__(self, eng, s, base=0, gated=False, between=None):
                self.eng, self.s, self.base, self.n, self.gated = eng, s, base, 0, gated
                self.between = between

            def inc(self, ins):
                self.n += 1
                ins.then_inc(self.s, 1)

            def wait(self):
                self.eng.wait_ge(self.s, self.base + self.n)
                if self.gated:
                    gate(self.eng)

            def __call__(self, ins):
                self.inc(ins)
                if self.between:
                    next(self.between, None)
                self.wait()

        def gate(eng):
            eng.sem_inc(gates, 1)

        def col(ap, at, n=1):
            return ap[:, bass.ds(at, n)]

        def tiles_of(ap3, t, n=1):
            return ap3[:, bass.ds(t, n), :]

        def head_of(ap):
            return ap[0:HEAD * P, :].rearrange("(t p) d -> p t d", p=P)

        def tail_of(ap):
            return ap[HEAD * P:N, :].rearrange("(p t) d -> p t d", p=P)

        adj_head = adj_d[0:HEAD * P, :].rearrange("(t p) n -> t p n", p=P)
        adj_tail = adj_d[HEAD * P:N, :].rearrange("(p t) n -> t p n", p=P)

        def rows_dma(eng, to_dram, ap_d, ap3, s):
            for part, view in ((slice(0, HEAD), head_of(ap_d)), (slice(HEAD, NT), tail_of(ap_d))):
                a, b = (view, ap3[:, part, :]) if to_dram else (ap3[:, part, :], view)
                eng.dma_start(a, b).then_inc(s, 16)

        def scores_of(tile):
            return big_scores if tile.static == 0 else scores[tile.ring][:, 0:tile.chunks * P]

        def buffers_of(tile, k):
            b = (tile.segment_static + k) % 2
            return s2_ps[b], slopes_of[b], masks_of[b]

        def diagonal_of(L, tile, k):
            return (diagonal, keys)[(tile.segment_static + k) % 2] if L.n else diagonal

        def place_of_group(tile, k):
            return (range(4 * k, min(4 * k + 4, tile.chunks)), probsT[(tile.group_static + k) % 2])

        @block.sync
        def _(sp):
            def load_tile(w):
                cur = w.back(0)
                if cur:
                    if cur.static >= 2:
                        sp.wait_ge(casts, cur.t * 2 - 2)
                    src = adj_head[w.s] if w.s < HEAD else adj_tail[w.i * UNROLL + (w.s - HEAD)]
                    sp.dma_start(adj[cur.par][:, :], src).then_inc(adj_in[cur.par], 16)
                done = w.back(19)
                if done and w.s % 2:
                    sp.wait_ge(dots_made, done.pair * 4 + 4)
                    src = table3[:, bass.ds(done.t, 2), 0:RG]
                    if done.static < HEAD:
                        dst = head_of(table_d[1])[:, done.static:done.static + 2, :]
                    else:
                        dst = tail_of(table_d[1])[:, bass.ds(w.i * UNROLL + (done.static - HEAD), 2), :]
                    sp.dma_start(dst, src).then_inc(pair_out, 16)

            def dense_loads(L, B):
                sp.wait_ge(B.rows, NT // 4)
                with nc.allow_non_contiguous_dma(reason="one column, on the dense path alone"):
                    rows_dma(sp, True, s2_d[L.n], table3[:, :, D:D + 1], L.s2)
                sp.wait_ge(L.s2, 32)
                sp.dma_start(s2_row, s2_d[L.n].rearrange("n one -> one n").to_broadcast((P, N))
                             ).then_inc(L.s2, 16)
                for t in range(HEAD):
                    if t:
                        sp.wait_ge(L.done, t)
                    sp.dma_start(adj[0][:, :], adj_head[t]).then_inc(L.adj, 16)
                with sp.Fori(0, TAIL) as i:
                    sp.wait_ge(L.done, i + HEAD)
                    sp.dma_start(adj[0][:, :], adj_tail[i]).then_inc(L.adj, 16)

            rows_dma(sp, False, x_d, x3, x_in)
            sp.dma_start(w_sb[:, 0:D], w_d).then_inc(w_in, 16)
            for n, a_d in enumerate((a0_d, a1_d)):
                sp.dma_start(a_sb[:, 2 * n:2 * n + 1], a_d[D:2 * D, :]).then_inc(w_in, 16)
                sp.dma_start(a_sb[:, 2 * n + 1:2 * n + 2], a_d[0:D, :]).then_inc(w_in, 16)
            sp.dma_start(a_row[:, :], a1_d.rearrange("n one -> one n").to_broadcast((P, 2 * D))
                         ).then_inc(w_in, 16)

            def step(w):
                load_tile(w)
                if w.s == 2:
                    sp.wait_ge(first_table.rows, NT // 4)
                    rows_dma(sp, True, table_d[0], table3[:, :, 0:RG], first_table.stored)

            each_step(sp, NT, 19, step)
            sp.wait_ge(pair_out, NT // 2 * 16)
            sp.wait_ge(flag_made, 1)
            dense = sp.value_load(flag[0:1, 0:1], min_val=0, max_val=1)
            with sp.If(dense < 1):
                def store(w):
                    done = w.back(3)
                    if done and w.s % RING == RING - 1:
                        sp.wait_ge(out_pairs, done.pair + 2)
                        src = x3[:, bass.ds(done.t, RING), :]
                        if done.static < HEAD:
                            dst = head_of(out_d)[:, done.static:done.static + RING, :]
                        else:
                            dst = tail_of(out_d)[:, bass.ds(w.i * UNROLL + (done.static - HEAD), RING), :]
                        sp.dma_start(dst, src).then_inc(out_in, 16)

                each_step(sp, NT, 3, store)
                sp.wait_ge(out_in, NT // RING * 16)
            with sp.If(dense > 0):
                rows_dma(sp, False, x_d, x3, x_again)
                for L, B in zip(dense_layers, dense_tables):
                    dense_loads(L, B)
                    sp.wait_ge(L.post, 1)
                    if L.n == 0:
                        rows_dma(sp, False, x_d, by_tile(x_b), L.x_in)
                        sp.wait_ge(L.x_out, 1)
                        sp.dma_start(x1_d, agg[:, :]).then_inc(L.x_in, 16)
                        sp.wait_ge(L.x_in, 48)
                    else:
                        sp.dma_start(x_b, x1_d).then_inc(L.x_in, 16)
                        sp.wait_ge(L.x_out, 1)
                        rows_dma(sp, True, out_d, agg3, L.x_in)
                        sp.wait_ge(L.x_in, 48)

        @block.gpsimd
        def _(pool):
            G = nc.gpsimd

            def make_consts():
                G.memset(identity[:, :], 0.0).then_inc(consts, 1)
                G.memset(before[:, :], 1.0).then_inc(consts, 1)
                pool.wait_ge(consts, 2)
                G.affine_select(out=identity[:, :], in_=identity[:, :], compare_op=ALU.not_equal, fill=1.0,
                                base=0, pattern=[[-1, P]], channel_multiplier=1).then_inc(consts, 1)
                G.affine_select(out=before[:, :], in_=before[:, :], compare_op=ALU.is_gt, fill=0.0,
                                base=0, pattern=[[1, P]], channel_multiplier=-1).then_inc(consts, 1)
                G.iota(word_no[:, :], [[1, WORDS]], base=-OFFSET, channel_multiplier=0,
                       allow_small_or_imprecise_dtypes=True).then_inc(consts, 1)
                G.iota(edge_no[:, :], [[1, KMAX + EMAX]], base=-KMAX, channel_multiplier=0,
                       allow_small_or_imprecise_dtypes=True).then_inc(consts, 1)
                G.memset(halves[:, :], 0.5).then_inc(consts, 1)
                G.memset(ones[:, :], 1.0).then_inc(consts, 1)
                G.memset(quarters[:, :], 0.25).then_inc(consts, 1)

            def gather(L, cur):
                if cur.static >= ROWS:
                    pool.wait_ge(L.group_summed, cur.groups_until(ROWS))
                G.tensor_copy(index[cur.slot][:, 0:cur.chunks], col(index_all, cur.chunk, cur.chunks)
                              ).then_inc(L.index_copied, 1)
                pool.wait_ge(L.index_copied, cur.t + 1)
                gate(pool)
                for c in range(cur.chunks):
                    G.indirect_dma_start(
                        rows[cur.slot][:, c * RG:(c + 1) * RG], None, table_d[L.n],
                        bass.IndirectOffsetOnAxis(ap=index[cur.slot][:, c:c + 1], axis=0)
                    ).then_inc(L.rows_in[cur.slot], 16)

            def diagonals(L, t):
                pool.wait_ge(L.rows_in[t.slot], (t.slot_chunks + t.chunks) * 16)
                gate(pool)
                for k, (u, c0, e0, n) in enumerate(t.segments):
                    if t.static or k:
                        pool.wait_ge(L.s2_spread, t.segment + k)
                        gate(pool)
                    s2 = by_tile(rows[t.slot][:, c0 * RG:(c0 + n) * RG], RG)[:, :, D:D + 1]
                    G.tensor_tensor(by_tile(diagonal[:, 0:n * P], P), s2.to_broadcast((P, n, P)),
                                    identity[:, :].unsqueeze(1).to_broadcast((P, n, P)), ALU.mult
                                    ).then_inc(L.diagonal_made, 1)

            def reach_of(cur):
                n = len(cur.units)
                c = Steps(pool, pool_m, cur.t * 4, gated=True)
                count, first, half, mid, far = (
                    col(a, cur.unit, n) for a in (count_all, first_all, half_count, middle, reach))
                pool.wait_ge(firsts, cur.t + 1)
                gate(pool)
                c(G.tensor_tensor(half, count, halves[:, 0:n], ALU.mult))
                c.inc(G.tensor_tensor(far, half, quarters[:, 0:n], ALU.subtract))
                c(G.tensor_tensor(mid, halves[:, 0:n], half, ALU.subtract))
                c.inc(G.tensor_tensor(mid, mid, first, ALU.subtract))

            def sums(a):
                c = Steps(pool, pool_1, a.pair * 3, gated=True)
                wide = (P, 2, D)
                r = a.ring
                pool.wait_ge(layers[0].copied, a.t + 2)
                pool.wait_ge(recs, a.pair * 3 + 3)
                gate(pool)
                if a.static >= 2:
                    pool.wait_ge(x1_made, a.pair)
                    gate(pool)
                G.tensor_tensor(by_tile(pair_a[:, :]), acc3[:, r:r + 2, :],
                                rec[:, :].unsqueeze(2).to_broadcast(wide), ALU.mult).then_inc(pool_1, 1)
                G.tensor_tensor(by_tile(pair_b[:, :]), no_edge[:, :].unsqueeze(2).to_broadcast(wide),
                                mean_row[0][:, :].unsqueeze(1).to_broadcast(wide), ALU.mult
                                ).then_inc(pool_1, 1)
                c.n = 2
                c.wait()
                c(G.tensor_tensor(pair_a[:, :], pair_a[:, :], pair_b[:, :], ALU.add))
                G.tensor_scalar(pair_b[:, :], pair_a[:, :], 0.0, None, ALU.min).then_inc(neg_made, 1)

            def residual(a):
                c = Steps(pool, pool_2, a.pair * 3, gated=True)
                pool.wait_ge(exp_made, a.pair + 1)
                gate(pool)
                c.inc(G.tensor_scalar(pair_b[:, :], pair_b[:, :], -1.0, None, ALU.add))
                c(G.tensor_scalar(pair_a[:, :], pair_a[:, :], 0.0, None, ALU.max))
                c(G.tensor_tensor(pair_a[:, :], pair_a[:, :], pair_b[:, :], ALU.add))
                G.tensor_tensor(tiles_of(x3, a.t, 2), by_tile(pair_a[:, :]), tiles_of(x3, a.t, 2), ALU.add
                                ).then_inc(x1_made, 1)

            def step(w):
                if w.back(2):
                    pool.wait_ge(indexed, w.back(2).t + 1)
                    gather(layers[0], w.back(2))
                if w.back(3):
                    diagonals(layers[0], w.back(3))
                if w.s % 2 and w.back(9):
                    residual(w.back(9))
                if w.s % 2 and w.back(7):
                    sums(w.back(7))
                if w.back(1):
                    reach_of(w.back(1))

            def step2(w):
                if w.back(0):
                    gather(layers[1], w.back(0))

            make_consts()
            pool.wait_ge(first_table.stored, 32)
            each_step(pool, NT, 9, step)
            pool.wait_ge(flag_made, 1)
            dense = pool.value_load(flag[0:1, 0:1], min_val=0, max_val=1)
            with pool.If(dense < 1):
                pool.wait_ge(pair_out, NT // 2 * 16)
                each_step(pool, NT, ROWS, step2)

        @block.scalar
        def _(act):
            A = nc.scalar

            def roots(B, n, centred3, square3):
                for k in range(n + 1):
                    if k < n:
                        at = slice(k * (NT // n), (k + 1) * (NT // n))
                        act.wait_ge(B.centred, k + 1)
                        A.activation(square3[:, at, :], centred3[:, at, :], ACT.Square).then_inc(B.squared, 1)
                    if k:
                        at = slice((k - 1) * (NT // n), k * (NT // n))
                        act.wait_ge(B.var, k)
                        A.activation(stat[:, NT:2 * NT][:, at], stat[:, 0:NT][:, at], ACT.Ln, bias=eps[:, :]
                                     ).then_inc(B.act, 1)
                        act.wait_ge(B.act, k)
                        A.activation(stat[:, 2 * NT:3 * NT][:, at], stat[:, NT:2 * NT][:, at], ACT.Exp,
                                     scale=-0.5).then_inc(B.root, 1)

            def turn_weights(B):
                act.wait_ge(B.wT_ps, 1)
                A.copy(wT[:, :], sum_ps[0:D, 0:D]).then_inc(B.wT, 1)
                act.wait_ge(B.wa_ps, 1)
                A.copy(w_sb[:, D:R], sum_ps[0:D, 64:66]).then_inc(B.wa, 1)

            def make_table(B):
                for q in range(NT // 4 + 1):
                    if q < NT // 4:
                        act.wait_ge(B.hT_ps, q + 1)
                        if q >= 2:
                            act.wait_ge(B.rows_ps, q - 1)
                        A.copy(hT[q % 2][:, :], hT_ps[q % 2][0:D, :]).then_inc(B.hT, 1)
                    if q:
                        act.wait_ge(B.rows_ps, q)
                        four, ps_q = slice(4 * q - 4, 4 * q), rows_ps[(q - 1) % 2]
                        if B.layer == 0:
                            A.copy(table3[:, four, :], by_tile(ps_q[:, 0:4 * R], R)).then_inc(B.rows, 1)
                        else:
                            A.copy(table3[:, four, D:R], by_tile(ps_q[:, 0:8], 2)).then_inc(B.rows, 1)

            def mean(B):
                act.wait_ge(B.mean_ps, 1)
                A.mul(mean_row[B.layer][:, :], sum_ps[:, 0:D], 1.0 / N).then_inc(B.mean, 1)

            def cast(cur, h):
                if h == 0:
                    act.wait_ge(adj_in[cur.par], cur.pair * 16 + 16)
                    if cur.static >= 2:
                        act.wait_ge(counted, cur.t - 1)
                if cur.static >= 1:
                    act.wait_ge(packs, cur.t * 2 - 1 + h)
                gate(act)
                A.activation(signs[h][:, :], adj[cur.par][:, h * HALF:(h + 1) * HALF], ACT.Sign,
                             accum_out=degree[cur.par][:, h:h + 1]).then_inc(casts, 1)

            def probs(L, t):
                act.wait_ge(L.shifted, t.t + 1)
                if t.static >= RING:
                    if L.n == 0:
                        act.wait_ge(recs, t.pair * 3 - 3)
                    else:
                        act.wait_ge(out_pairs, t.pair - 1)
                gate(act)
                sc = scores_of(t)
                A.activation(sc, sc, ACT.Exp, bias=shift[t.par][:, :],
                             accum_out=den[:, t.ring:t.ring + 1]).then_inc(L.probs, 1)

            def diagonals(L, t, k):
                u, c0, e0, n = t.segments[k]
                if k == 0:
                    act.wait_ge(L.rows_in[t.slot], (t.slot_chunks + t.chunks) * 16)
                if t.segment_static + k >= 2:
                    act.wait_ge(L.s2_spread, t.segment + k - 1)
                gate(act)
                for c in range(n):
                    at = (c0 + c) * RG + D
                    last = A.activation(diagonal_of(L, t, k)[:, c * P:(c + 1) * P], identity[:, :], ACT.Copy,
                                        scale=rows[t.slot][:, at:at + 1])
                last.then_inc(L.diagonal_made, 1)

            def slopes(L, t, k):
                u, c0, e0, n = t.segments[k]
                g, w = t.segment + k, n * P
                s2, slope, mask = buffers_of(t, k)
                if t.segment_static + k >= 2:
                    act.wait_ge(L.masked, g - 1)
                act.wait_ge(L.s2_spread, g + 1)
                gate(act)
                A.activation(slope[:, 0:w], s2[:, 0:w], ACT.Identity, bias=col(s1_slope[L.n], t.t),
                             scale=ALPHA).then_inc(L.slope_made, 1)
                A.activation(mask[:, 0:w], edge_no[:, KMAX + e0:KMAX + e0 + w], ACT.Abs,
                             bias=col(middle, t.unit + u)).then_inc(L.distance_made, 1)

            def copy_turned(L, t, k):
                chunks, buffer = place_of_group(t, k)
                n = len(chunks) * P
                act.wait_ge(L.turned, t.group + (k + 1))
                if t.group_static + k >= 2:
                    act.wait_ge(L.group_summed, t.group + k - 1)
                gate(act)
                A.copy(buffer[:, 0:n], turned_ps[:, 0:n]).then_inc(L.turned_copied, 1)

            def step(w):
                L, B = layers[0], first_table
                cur, t3, t5 = w.back(0), w.back(3), w.back(5)
                if cur:
                    cast(cur, 0)
                if t5:
                    probs(L, t5)
                if cur:
                    cast(cur, 1)
                if t3:
                    act.wait_ge(pool_m, t3.t * 4 + 4)
                    gate(act)
                    slopes(L, t3, 0)
                if t5:
                    copy_turned(L, t5, 0)
                if t3:
                    for k in range(1, len(t3.segments)):
                        slopes(L, t3, k)
                if t5:
                    for k in range(1, t5.groups):
                        copy_turned(L, t5, k)
                if w.s == 0:
                    make_table(B)
                    act.wait_ge(B.rows, NT // 4)
                    A.mul(s1_slope[0][:, :], table3[:, :, D + 1], ALPHA).then_inc(s1_made, 1)
                    A.copy(s1[0][:, :], table3[:, :, D + 1]).then_inc(s1_made, 1)
                    act.wait_ge(s1_made, 2)
                if w.s == 3:
                    mean(B)
                if w.s % 2 and w.back(9):
                    a = w.back(9)
                    act.wait_ge(neg_made, a.pair + 1)
                    A.activation(pair_b[:, :], pair_b[:, :], ACT.Exp).then_inc(exp_made, 1)
                if w.s % 2 == 0 and w.back(12):
                    a = w.back(12)
                    root = root2[a.ring // 2][:, :]
                    act.wait_ge(var_made, a.pair + 1)
                    if a.static >= 4:
                        act.wait_ge(root_step, a.pair * 6 - 6)
                    gate(act)
                    A.activation(root, aggr[a.ring // 2][:, :].rearrange("p (t v) -> p t v", v=2)[:, :, 1],
                                 ACT.Ln, bias=eps[:, :]).then_inc(act_r, 1)
                    act.wait_ge(act_r, a.pair + 1)
                    A.activation(root, root, ACT.Exp, scale=-0.5).then_inc(root_made, 1)
                if w.s % 2 == 0 and w.back(14):
                    a = w.back(14)
                    if a.static == 0:
                        act.wait_ge(B.stored, 32)
                    act.wait_ge(root_step, a.pair * 6 + 6)
                    gate(act)
                    for k in range(2):
                        A.activation(table3[:, bass.ds(a.t + k, 1), 0:D], x3[:, bass.ds(a.t + k, 1), :],
                                     ACT.Relu, bias=pair_s[a.ring // 2][:, 2 + k:3 + k],
                                     scale=pair_s[a.ring // 2][:, k:k + 1]).then_inc(h_made, 1)

            def step2(w):
                L = layers[1]
                t2, t3, t5 = w.back(2), w.back(3), w.back(5)
                if t5:
                    probs(L, t5)
                if t3:
                    for k in range(len(t3.segments)):
                        if k + 1 < len(t3.segments):
                            diagonals(L, t3, k + 1)
                        slopes(L, t3, k)
                if t2:
                    diagonals(L, t2, 0)
                if t5:
                    for k in range(t5.groups):
                        copy_turned(L, t5, k)
                if w.s == 2:
                    act.wait_ge(h_mean, 1)
                    A.mul(mean_row[1][:, :], sum_ps[:, 0:D], 1.0 / N).then_inc(h_total, 1)

            def dense_attend(L):
                with act.Fori(0, NT) as i:
                    act.wait_ge(L.shifted, i + 1)
                    gate(act)
                    A.activation(dense_scores, dense_scores, ACT.Exp, bias=shift[0][:, :],
                                 accum_out=den[:, 0:1]).then_inc(L.probs, 1)

            act.preload_act_table_set("natural_log_exp_and_others")
            B = first_table
            act.wait_ge(dve_c, 1)
            roots(B, PIECES, agg3, table3[:, :, 0:D])
            turn_weights(B)
            each_step(act, NT, 14, step)
            act.wait_ge(flag_made, 1)
            dense = act.value_load(flag[0:1, 0:1], min_val=0, max_val=1)
            with act.If(dense < 1):
                act.wait_ge(dots_made, NT // 2 * 4)
                A.mul(s1_slope[1][:, :], s1[1][:, :], ALPHA).then_inc(s1_made, 1)
                act.wait_ge(s1_made, 3)
                each_step(act, NT, 5, step2)
            with act.If(dense > 0):
                for L, B in zip(dense_layers, dense_tables):
                    roots(B, 1, by_tile(centred_b), by_tile(square_b))
                    if L.n == 0:
                        turn_weights(B)
                    make_table(B)
                    mean(B)
                    dense_attend(L)
                    if L.n == 0:
                        act.wait_ge(L.neg, 1)
                        A.activation(exp_b, exp_b, ACT.Exp).then_inc(L.exp, 1)

        @block.vector
        def _(dve):
            V = nc.vector

            def make_consts():
                c = Steps(dve, dve_c)
                c.inc(V.memset(eps[:, :], EPS))
                at = 0
                for t in range(HEAD):
                    for _, chunks in units_of(t):
                        c.inc(V.memset(room[:, at:at + 1], float(chunks * P)))
                        at += 1
                c.inc(V.memset(room[:, at:NU], float(TAIL_UNITS[0][1] * P)))
                dve.wait_ge(consts, 9)
                for b in range(BITS):
                    c.inc(V.tensor_scalar(weights[:, b * P:(b + 1) * P], identity[:, :], float(1 << b),
                                          None, ALU.mult))
                c.wait()
                return c.n

            def normalise(B, n, src3, centred3, square3, out3):
                c, m = Steps(dve, B.step), NT // n
                wide = (P, m, D)

                def centre(k):
                    at = slice(k * m, (k + 1) * m)
                    mean = stat[:, 4 * NT:5 * NT][:, at]
                    c(V.tensor_reduce(mean, src3[:, at, :], AX.X, ALU.add))
                    c(V.tensor_scalar(mean, mean, 1.0 / D, None, ALU.mult))
                    V.tensor_tensor(centred3[:, at, :], src3[:, at, :], mean.unsqueeze(2).to_broadcast(wide),
                                    ALU.subtract).then_inc(B.centred, 1)

                def variance(k):
                    at = slice(k * m, (k + 1) * m)
                    var, v = stat[:, 0:NT][:, at], stat[:, 4 * NT:5 * NT][:, at]
                    dve.wait_ge(B.squared, k + 1)
                    c(V.tensor_reduce(var, square3[:, at, :], AX.X, ALU.add))
                    V.tensor_scalar(var, var, 1.0 / D, None, ALU.mult).then_inc(B.var, 1)
                    dve.wait_ge(B.var, k + 1)
                    dve.wait_ge(B.centred, k + 1)
                    c(V.tensor_scalar(v, var, EPS, None, ALU.add))

                def scale(k):
                    at = slice(k * m, (k + 1) * m)
                    y, z, v = (stat[:, j * NT:(j + 1) * NT][:, at] for j in (2, 3, 4))
                    dve.wait_ge(B.root, k + 1)
                    c(V.tensor_tensor(z, y, y, ALU.mult))
                    c(V.tensor_tensor(z, z, v, ALU.mult))
                    c(V.tensor_scalar(z, z, -0.5, 1.5, ALU.mult, ALU.add))
                    c(V.tensor_tensor(z, y, z, ALU.mult))
                    V.scalar_tensor_tensor(out=out3[:, at, :], in0=centred3[:, at, :], scalar=0.0,
                                           in1=z.unsqueeze(2).to_broadcast(wide), op0=ALU.max,
                                           op1=ALU.mult).then_inc(B.h, 1)

                for k in range(n + 2):
                    for stage, j in ((centre, k), (variance, k - 1), (scale, k - 2)):
                        if 0 <= j < n:
                            stage(j)

            def take(cur, between):
                c = Steps(dve, dve_t, cur.take_step, between=between)
                rounds = word_rounds_of(cur.static)
                n, levels = 8 * rounds, cur.levels
                dve.wait_ge(packs, cur.t * 2 + 2)
                c(V.scalar_tensor_tensor(out=keys[:, :], in0=packed[cur.par][:, :], scalar=float(WORDS),
                                         in1=word_no[:, :], op0=ALU.mult, op1=ALU.add))
                src = keys
                for r in range(rounds):
                    best = found[:, 8 * r:8 * r + 8]
                    gate(dve)
                    c(V.max(best, src[:, :]))
                    if r < rounds - 1:
                        gate(dve)
                        dst = kept if src is keys else keys
                        c(V.match_replace(dst[:, :], best, src[:, :], USED))
                        src = dst
                f_i = found_i[:, 0:n]
                c(V.tensor_copy(f_i, found[:, 0:n]))
                c(V.tensor_scalar(f_i, f_i, OFFSET, 2 * OFFSET - 1, ALU.bitwise_xor, ALU.bitwise_and))
                c.inc(V.tensor_scalar(word_of[:, 0:n], f_i, WORDS - 1, None, ALU.bitwise_and))
                c(V.tensor_scalar(bits_i[:, 0:n], f_i, WORDS.bit_length() - 1, None,
                                  ALU.logical_shift_right))
                c(V.tensor_copy(bits[:, 0:n], bits_i[:, 0:n]))
                b_i = bits[:, 0:n].bitcast(I32)
                for level in range(levels):
                    if cur.static == 0:
                        out = ranked[:, 0:n] if level == 0 else lower[:, (level - 1) * n:level * n]
                    else:
                        out = lower[:, level * n:(level + 1) * n]
                    c.inc(V.scalar_tensor_tensor(out=out.bitcast(I32), in0=b_i, scalar=EXPONENT,
                                                 in1=word_of[:, 0:n], op0=ALU.bitwise_and,
                                                 op1=ALU.bitwise_or))
                    if level < levels - 1:
                        c(V.tensor_scalar(top_bit[:, 0:n].bitcast(I32), b_i, EXPONENT, None,
                                          ALU.bitwise_and))
                        c(V.tensor_tensor(bits[:, 0:n], bits[:, 0:n], top_bit[:, 0:n], ALU.subtract))
                c.wait()
                m = (levels - (cur.static == 0)) * n
                c(V.tensor_scalar(lower[:, 0:m], lower[:, 0:m], 0.25, None, ALU.max))
                last_rounds = cur.units[-1][0]
                at = n if cur.static == 0 else 0
                for r in range(last_rounds):
                    best = ranked[:, at + 8 * r:at + 8 * r + 8]
                    gate(dve)
                    c(V.max(best, lower[:, 0:m]))
                    if r < last_rounds - 1:
                        gate(dve)
                        c(V.match_replace(lower[:, 0:m], best, lower[:, 0:m], 0.25))
                n = cur.slots
                pairs = values[cur.par][:, 0:2 * n].rearrange("p (k v) -> p k v", v=2)
                r_i = ranked[:, 0:n].bitcast(I32)
                c.inc(V.tensor_scalar(exponent[:, 0:n], r_i, 23 - (WORDS.bit_length() - 1), ((1 << 9) - 1) * WORDS,
                                      ALU.logical_shift_right, ALU.bitwise_and))
                c(V.tensor_scalar(column[:, 0:n], r_i, WORDS - 1, None, ALU.bitwise_and))
                if cur.static >= 2:
                    dve.wait_ge(edged, cur.unit - len(units_of(cur.static - 1)))
                c(V.tensor_scalar(pairs[:, :, 1], exponent[:, 0:n], 126.0 * WORDS, 0.0, ALU.subtract, ALU.max))
                k, nu = 0, len(cur.units)
                for u, (r, _) in enumerate(cur.units):
                    c.inc(V.tensor_scalar(valid[:, k:k + 8 * r], pairs[:, k:k + 8 * r, 1], 0.5, None,
                                          ALU.is_ge, ALU.add, accum_out=col(count_all, cur.unit + u)))
                    k += 8 * r
                c.wait()
                c.inc(V.tensor_tensor(pairs[:, :, 0], column[:, 0:n], valid[:, 0:n], ALU.mult))
                found_n = col(count_all, cur.unit)
                if nu > 1:
                    found_n = total[:, 0:1]
                    c(V.tensor_reduce(found_n, col(count_all, cur.unit, nu), AX.X, ALU.add))
                d = degree[cur.par]
                V.scalar_tensor_tensor(out=col(missed, cur.t), in0=d[:, 0:1], scalar=d[:, 1:2],
                                       in1=found_n, op0=ALU.add, op1=ALU.subtract).then_inc(counted, 1)
                assert c.n == take_steps(cur.static), (cur.static, c.n, take_steps(cur.static))

            def index_of(t):
                dve.wait_ge(edged, t.unit + len(t.units))
                if t.static:
                    dve.wait_ge(indexed, t.t)
                n = t.chunks
                e = edges_ps[:, 0:2 * n].rearrange("p (c v) -> p c v", v=2)
                V.tensor_reduce(edge_f[:, 0:n], e, AX.X, ALU.add).then_inc(dve_i, 1)
                yield
                dve.wait_ge(dve_i, t.t + 1)
                V.tensor_scalar(col(index_all, t.chunk, n), edge_f[:, 0:n], float(-WORDS), 0.0, ALU.add,
                                ALU.max).then_inc(indexed, 1)
                yield

            def place_of(cur):
                nu = len(cur.units)
                dve.wait_ge(summed, cur.t + 1)
                V.tensor_copy(col(first_all, cur.unit, nu), starts_ps[:, 0:nu]).then_inc(firsts, 1)
                dve.wait_ge(firsts, cur.t + 1)
                for u, (r, chunks) in enumerate(cur.units):
                    if cur.static or u:
                        dve.wait_ge(edged, cur.unit + u)
                    V.tensor_scalar(place[:, 0:8 * r + chunks * P],
                                    edge_no[:, KMAX - 8 * r:KMAX + chunks * P],
                                    col(first_all, cur.unit + u), None, ALU.is_equal).then_inc(placed, 1)

            def score(L, cur):
                sc = scores_of(cur)
                for k, (u, c0, e0, n) in enumerate(cur.segments):
                    g, w = cur.segment + k, n * P
                    s2, slope, mask = buffers_of(cur, k)
                    dve.wait_ge(L.slope_made, g + 1)
                    V.scalar_tensor_tensor(out=leaky[:, 0:w], in0=s2[:, 0:w], scalar=col(s1[L.n], cur.t),
                                           in1=slope[:, 0:w], op0=ALU.add, op1=ALU.max
                                           ).then_inc(L.s2_read, 1)
                    yield
                    dve.wait_ge(L.distance_made, g + 1)
                    V.tensor_scalar(mask[:, 0:w], mask[:, 0:w], col(reach, cur.unit + u), MASKED,
                                    ALU.is_gt, ALU.mult).then_inc(L.dve, 1)
                    yield
                    if k == 0 and cur.static >= RING:
                        dve.wait_ge(L.turned, cur.groups_until(RING))
                    if k == 0 and cur.static:
                        dve.wait_ge(L.shifted, cur.t)
                    dve.wait_ge(L.s2_read, g + 1)
                    dve.wait_ge(L.dve, cur.score_step + (k + 1))
                    gate(dve)
                    V.tensor_tensor_reduce(
                        out=sc[:, c0 * P:c0 * P + w], in0=leaky[:, 0:w], in1=mask[:, 0:w], scale=1.0,
                        scalar=FLOOR, op0=ALU.add, op1=ALU.max, accum_out=top[:, k:k + 1]
                    ).then_inc(L.masked, 1)
                    yield
                    dve.wait_ge(L.masked, g + 1)
                m = top[:, 0:1]
                if len(cur.segments) > 1:
                    m = top[:, 7:8]
                    V.tensor_reduce(m, top[:, 0:len(cur.segments)], AX.X, ALU.max).then_inc(L.dve, 1)
                    yield
                    dve.wait_ge(L.dve, cur.score_step + score_steps(cur.static))
                if cur.static >= 2:
                    dve.wait_ge(L.probs, cur.t - 1)
                V.tensor_scalar(shift[cur.par][:, :], m, -1.0, None, ALU.mult).then_inc(L.shifted, 1)
                yield

            def copy_sum(L, t):
                dve.wait_ge(L.group_summed, t.group + t.groups)
                if L.n == 0 and t.static >= RING:
                    dve.wait_ge(neg_made, t.pair - 1)
                V.tensor_copy(acc3[:, t.ring:t.ring + 1, :], sum_ps[:, 0:D].unsqueeze(1)
                              ).then_inc(L.copied, 1)

            def reciprocals(L, a, s, base):
                d = den[:, a.ring:a.ring + 2]
                dve.wait_ge(L.probs, a.t + 2)
                V.tensor_scalar(no_edge[:, :], d, 0.5, None, ALU.is_lt).then_inc(s, 1)
                yield
                dve.wait_ge(s, base + 1)
                V.tensor_tensor(rec[:, :], d, no_edge[:, :], ALU.add).then_inc(s, 1)
                yield
                dve.wait_ge(s, base + 2)
                V.reciprocal(rec[:, :], rec[:, :]).then_inc(s, 1)
                yield

            def variance(a):
                dve.wait_ge(x1_made, a.pair + 1)
                if a.static >= 4:
                    dve.wait_ge(root_step, a.pair * 6 - 6)
                if a.static:
                    dve.wait_ge(var_made, a.pair)
                gate(dve)
                for k in range(2):
                    V.bn_stats(stats[:, 6 * k:6 * k + 6], x3[:, bass.ds(a.t + k, 1), :]).then_inc(dve_v, 1)
                yield
                dve.wait_ge(dve_v, a.pair * 3 + 2)
                gate(dve)
                V.bn_aggr(aggr[a.ring // 2][:, 0:2], stats[:, 0:6]).then_inc(dve_v, 1)
                V.bn_aggr(aggr[a.ring // 2][:, 2:4], stats[:, 6:12]).then_inc(var_made, 1)
                yield

            def sharpen(a):
                scale, shifts = pair_s[a.ring // 2][:, 0:2], pair_s[a.ring // 2][:, 2:4]
                root = root2[a.ring // 2][:, :]
                mean, var = (aggr[a.ring // 2][:, :].rearrange("p (t v) -> p t v", v=2)[:, :, k] for k in range(2))
                base = a.pair * 6
                dve.wait_ge(root_made, a.pair + 1)
                if a.static >= 4:
                    dve.wait_ge(h_made, a.pair * 2 - 2)
                if a.static:
                    dve.wait_ge(root_step, base)
                V.tensor_scalar(var_eps[:, :], var, EPS, None, ALU.add).then_inc(root_step, 1)
                V.tensor_tensor(scale, root, root, ALU.mult).then_inc(root_step, 1)
                yield
                dve.wait_ge(root_step, base + 2)
                V.tensor_tensor(scale, scale, var_eps[:, :], ALU.mult).then_inc(root_step, 1)
                yield
                dve.wait_ge(root_step, base + 3)
                V.tensor_scalar(scale, scale, -0.5, 1.5, ALU.mult, ALU.add).then_inc(root_step, 1)
                yield
                dve.wait_ge(root_step, base + 4)
                V.tensor_tensor(scale, scale, root, ALU.mult).then_inc(root_step, 1)
                yield
                dve.wait_ge(root_step, base + 5)
                V.scalar_tensor_tensor(out=shifts, in0=mean, scalar=-1.0, in1=scale, op0=ALU.mult,
                                       op1=ALU.mult).then_inc(root_step, 1)
                yield

            def dot(a):
                dve.wait_ge(h_made, a.pair * 2 + 2)
                for k in range(2):
                    for j, out in enumerate((s1[1][:, bass.ds(a.t + k, 1)],
                                             table3[:, bass.ds(a.t + k, 1), D])):
                        n = 2 * k + j
                        if a.static or n:
                            dve.wait_ge(dots_made, a.pair * 4 + n)
                        V.scalar_tensor_tensor(
                            out=dots[:, :].unsqueeze(1), in0=table3[:, bass.ds(a.t + k, 1), 0:D], scalar=1.0,
                            in1=a_row[:, j * D:(j + 1) * D].unsqueeze(1), op0=ALU.mult, op1=ALU.mult,
                            accum_out=out).then_inc(dots_made, 1)
                        yield

            def others(w):
                L = layers[0]
                if w.back(3):
                    if w.s == 3:
                        dve.wait_ge(s1_made, 2)
                    yield from score(L, w.back(3))
                if w.back(1):
                    yield from index_of(w.back(1))
                if w.s % 2 == 0 and w.back(6):
                    a = w.back(6)
                    if a.static >= 2:
                        dve.wait_ge(neg_made, a.pair)
                    yield from reciprocals(L, a, recs, a.pair * 3)
                if w.s % 2 == 0 and w.back(10):
                    yield from variance(w.back(10))
                if w.s % 2 == 0 and w.back(12):
                    yield from sharpen(w.back(12))
                if w.s % 2 and w.back(15):
                    yield from dot(w.back(15))
                if w.back(5):
                    copy_sum(L, w.back(5))

            def sum_columns(B):
                dve.wait_ge(B.rows, NT // 4)
                V.tensor_reduce(h_sum[:, 0:D], table3[:, :, 0:D].rearrange("p t d -> p d t"), AX.X,
                                ALU.add).then_inc(B.summed, 1)

            def step(w):
                if w.s == 2:
                    sum_columns(first_table)
                pieces = others(w)
                if w.back(0):
                    take(w.back(0), pieces)
                for _ in pieces:
                    pass
                if w.back(0):
                    place_of(w.back(0))

            def judge():
                c = Steps(dve, dve_f)
                dve.wait_ge(counted, NT)
                dve.wait_ge(firsts, NT)
                c.inc(V.tensor_reduce(fault[:, 0:1], missed[:, :], AX.X, ALU.max,
                                      apply_absolute_value=True))
                c(V.tensor_tensor(half_count[:, :], first_all[:, :], count_all[:, :], ALU.add))
                c(V.tensor_tensor(half_count[:, :], half_count[:, :], room[:, :], ALU.subtract))
                c.inc(V.tensor_reduce(fault[:, 1:2], half_count[:, :], AX.X, ALU.max))
                c(V.memset(fault[:, 3:4], 1.0))
                V.tensor_scalar(fault[:, 2:3], fault[:, 0:1], fault[:, 1:2], 0.0, ALU.max, ALU.is_gt
                                ).then_inc(fault_made, 1)
                dve.wait_ge(fault_sum, 1)
                V.tensor_scalar(flag[0:1, 0:1], edges_ps[0:1, 256:257], 0.0, None, ALU.is_gt
                                ).then_inc(flag_made, 1)
                dve.wait_ge(flag_made, 1)

            out_step = sem("dve_out_step")

            def finish(a):
                wide = (P, 2, D)
                base = a.pair * 6
                dve.wait_ge(layers[1].copied, a.t + 2)
                if a.static:
                    dve.wait_ge(out_pairs, a.pair)
                yield from reciprocals(layers[1], a, out_step, base)
                V.tensor_tensor(by_tile(pair_b[:, :]), no_edge[:, :].unsqueeze(2).to_broadcast(wide),
                                mean_row[1][:, :].unsqueeze(1).to_broadcast(wide), ALU.mult
                                ).then_inc(out_step, 1)
                dve.wait_ge(out_step, base + 3)
                V.tensor_tensor(by_tile(pair_a[:, :]), acc3[:, a.ring:a.ring + 2, :],
                                rec[:, :].unsqueeze(2).to_broadcast(wide), ALU.mult).then_inc(out_step, 1)
                yield
                dve.wait_ge(out_step, base + 5)
                V.tensor_tensor(pair_a[:, :], pair_a[:, :], pair_b[:, :], ALU.add).then_inc(out_step, 1)
                yield
                dve.wait_ge(out_step, base + 6)
                x = tiles_of(x3, a.t, 2)
                V.scalar_tensor_tensor(out=x, in0=by_tile(pair_a[:, :]), scalar=0.0, in1=x, op0=ALU.max,
                                       op1=ALU.add).then_inc(out_pairs, 1)
                yield

            def step2(w):
                L = layers[1]
                if w.s == 1:
                    V.tensor_reduce(h_sum[:, 0:D], table3[:, :, 0:D].rearrange("p t d -> p d t"), AX.X,
                                    ALU.add).then_inc(h_summed, 1)
                pieces = iter(())
                if w.s % 2 and w.back(7):
                    pieces = finish(w.back(7))
                if w.back(3):
                    for _ in score(L, w.back(3)):
                        next(pieces, None)
                for _ in pieces:
                    pass
                if w.back(5):
                    copy_sum(L, w.back(5))

            def dense_attend(L):
                BLK = SEG * P
                dve.wait_ge(L.s2, 48)
                per_tile = 1 + 3 * (N // BLK) + 1 + 2
                slope = slopes_of[0]
                with dve.Fori(0, NT) as i:
                    c = Steps(dve, L.dve, i * per_tile)
                    dve.wait_ge(L.adj, i * 16 + 16)
                    c(V.tensor_scalar(dense_scores, adj[0][:, :], 0.0, MASKED, ALU.is_le, ALU.mult))
                    for k in range(N // BLK):
                        at = slice(k * BLK, (k + 1) * BLK)
                        c(V.tensor_scalar(slope[:, :], s2_row[:, at],
                                          table3[:, bass.ds(i, 1), D + 1], None, ALU.add))
                        c(V.scalar_tensor_tensor(out=leaky[:, :], in0=slope[:, :], scalar=ALPHA,
                                                 in1=slope[:, :], op0=ALU.mult, op1=ALU.max))
                        gate(dve)
                        c(V.tensor_tensor_reduce(
                            out=dense_scores[:, at], in0=leaky[:, :], in1=dense_scores[:, at],
                            scale=1.0, scalar=FLOOR, op0=ALU.add, op1=ALU.max,
                            accum_out=found[:, k:k + 1]))
                    c(V.tensor_reduce(top[:, 0:1], found[:, 0:N // BLK], AX.X, ALU.max))
                    V.tensor_scalar(shift[0][:, :], top[:, 0:1], -1.0, None, ALU.mult
                                    ).then_inc(L.shifted, 1)
                    for q in range(NT // 4):
                        dve.wait_ge(L.turned, i * (NT // 4) + (q + 1))
                        V.tensor_copy(probsT[0][:, :], turned_ps[:, :]).then_inc(L.copied, 1)
                    dve.wait_ge(L.summed, i + 1)
                    c.inc(V.tensor_copy(tiles_of(agg3, i), sum_ps[:, 0:D].unsqueeze(1)))
                    c.inc(V.tensor_copy(col(den_all, i), den[:, 0:1]))
                    c.wait()
                    dve.sem_inc(L.done, 1)
                    assert c.n == per_tile, c.n

            def dense_divide(L, c):
                none, r = stat[:, 0:NT], stat[:, NT:2 * NT]
                c(V.tensor_scalar(none, den_all[:, :], 0.5, None, ALU.is_lt))
                c(V.tensor_tensor(r, den_all[:, :], none, ALU.add))
                c(V.reciprocal(r, r))
                wide = (P, NT, D)
                c(V.tensor_tensor(agg3, agg3, r.unsqueeze(2).to_broadcast(wide), ALU.mult))
                c(V.tensor_tensor(by_tile(exp_b), none.unsqueeze(2).to_broadcast(wide),
                                  mean_row[L.n][:, :].unsqueeze(1).to_broadcast(wide), ALU.mult))
                c(V.tensor_tensor(agg[:, :], agg[:, :], exp_b, ALU.add))

            make_consts()
            dve.wait_ge(x_in, 32)
            normalise(first_table, PIECES, x3, agg3, table3[:, :, 0:D], agg3)
            each_step(dve, NT, 15, step)
            judge()
            dense = dve.value_load(flag[0:1, 0:1], min_val=0, max_val=1)
            with dve.If(dense < 1):
                each_step(dve, NT, 7, step2)
            with dve.If(dense > 0):
                dve.wait_ge(x_again, 32)
                normalise(dense_tables[0], 1, x3, by_tile(centred_b), by_tile(square_b), agg3)
                for L, B in zip(dense_layers, dense_tables):
                    sum_columns(B)
                    dve.wait_ge(B.mean, 1)
                    dense_attend(L)
                    c = Steps(dve, L.post)
                    dense_divide(L, c)
                    if L.n == 0:
                        dve.wait_ge(L.x_in, 32)
                        V.tensor_scalar(exp_b, agg[:, :], 0.0, None, ALU.min).then_inc(L.neg, 1)
                        dve.wait_ge(L.exp, 1)
                        c(V.scalar_tensor_tensor(out=agg[:, :], in0=exp_b, scalar=-1.0, in1=agg[:, :],
                                                 op0=ALU.add, op1=ALU.max))
                        c(V.tensor_tensor(agg[:, :], agg[:, :], x_b, ALU.add))
                        dve.sem_inc(L.x_out, 1)
                        normalise(dense_tables[1], 1, agg3, by_tile(centred_b), by_tile(square_b),
                                  table3[:, :, 0:D])
                        dve.wait_ge(L.x_in, 48)
                    else:
                        dve.wait_ge(L.x_in, 16)
                        V.scalar_tensor_tensor(out=agg[:, :], in0=agg[:, :], scalar=0.0, in1=x_b,
                                               op0=ALU.max, op1=ALU.add).then_inc(L.x_out, 1)

        @block.tensor
        def _(pe):
            T = nc.tensor

            def turn_weights(B):
                T.transpose(sum_ps[0:D, 0:D], w_sb[:, 0:D], identity[0:D, 0:D]).then_inc(B.wT_ps, 1)
                pe.wait_ge(B.wT, 1)
                T.matmul(sum_ps[0:D, 64:66], wT[:, :], a_sb[:, 0:2], start=True, stop=True
                         ).then_inc(B.wa_ps, 1)
                pe.wait_ge(B.wa, 1)

            def make_table(B, pieces):
                rhs, n = (w_sb[:, :], R) if B.layer == 0 else (a_sb[:, 2:4], 2)
                for q in range(NT // 4 + 1):
                    if q < NT // 4:
                        pe.wait_ge(B.h, q * pieces // (NT // 4) + 1)
                        if q >= 2:
                            pe.wait_ge(B.hT, q - 1)
                        for k in range(4):
                            t = 4 * q + k
                            h = agg3[:, t, :] if B.layer == 0 else table3[:, t, 0:D]
                            last = T.transpose(hT_ps[q % 2][0:D, k * P:(k + 1) * P], h, identity[:, :])
                        last.then_inc(B.hT_ps, 1)
                    if q:
                        b = (q - 1) % 2
                        pe.wait_ge(B.hT, q)
                        if q >= 3:
                            pe.wait_ge(B.rows, q - 2)
                        for k in range(4):
                            last = T.matmul(rows_ps[b][:, n * k:n * k + n], hT[b][:, k * P:(k + 1) * P],
                                            rhs, start=True, stop=True)
                        last.then_inc(B.rows_ps, 1)

            def mean(B):
                pe.wait_ge(B.summed, 1)
                T.matmul(sum_ps[:, 0:D], ones[:, :], h_sum[:, 0:D], start=True, stop=True
                         ).then_inc(B.mean_ps, 1)

            def words_of(cur, h):
                pe.wait_ge(casts, cur.t * 2 + (h + 1))
                if h == 0 and cur.static >= 2:
                    pe.wait_ge(counted, cur.t - 1)
                for b in range(BITS // 2):
                    bit = h * (BITS // 2) + b
                    last = T.matmul(packed[cur.par][:, :], weights[:, bit * P:(bit + 1) * P],
                                    signs[h][:, b * WORDS:(b + 1) * WORDS], start=(bit == 0),
                                    stop=(bit == BITS - 1))
                last.then_inc(packs, 1)

            def starts(t):
                pe.wait_ge(counted, t.t + 1)
                nu = len(t.units)
                T.matmul(starts_ps[:, 0:nu], before[:, :], col(count_all, t.unit, nu), start=True,
                         stop=True).then_inc(summed, 1)

            def pack_edges(t):
                slot, chunk = 0, 0
                for u, (r, chunks) in enumerate(t.units):
                    pe.wait_ge(placed, t.unit + (u + 1))
                    for c in range(chunks):
                        at = 2 * (chunk + c)
                        for k in range(8 * r):
                            src = 8 * r - k + c * P
                            last = T.matmul(edges_ps[:, at:at + 2], place[:, src:src + P],
                                            values[t.par][:, 2 * (slot + k):2 * (slot + k) + 2],
                                            start=(k == 0), stop=(k == 8 * r - 1))
                    last.then_inc(edged, 1)
                    slot += 8 * r
                    chunk += chunks

            def spread_s2(L, t, k):
                n = t.segments[k][3]
                if t.segment_static + k >= 2:
                    pe.wait_ge(L.s2_read, t.segment + k - 1)
                pe.wait_ge(L.diagonal_made, t.segment + (k + 1))
                T.matmul(buffers_of(t, k)[0][:, 0:n * P], ones[:, :], diagonal_of(L, t, k)[:, 0:n * P], start=True, stop=True
                         ).then_inc(L.s2_spread, 1)

            def turn_probs(L, t, k):
                if k == 0:
                    pe.wait_ge(L.probs, t.t + 1)
                if t.static or k:
                    pe.wait_ge(L.turned_copied, t.group + k)
                chunks, _ = place_of_group(t, k)
                sc = scores_of(t)
                for c in chunks:
                    last = T.transpose(turned_ps[:, (c % 4) * P:(c % 4 + 1) * P],
                                       sc[:, c * P:(c + 1) * P], identity[:, :])
                last.then_inc(L.turned, 1)

            def sum_rows(L, t):
                for k in range(t.groups):
                    if k + 1 < t.groups:
                        turn_probs(L, t, k + 1)
                    chunks, buffer = place_of_group(t, k)
                    pe.wait_ge(L.turned_copied, t.group + (k + 1))
                    if k == 0 and t.static:
                        pe.wait_ge(L.copied, t.t)
                    for c in chunks:
                        last = T.matmul(sum_ps[:, 0:D], buffer[:, (c % 4) * P:(c % 4 + 1) * P],
                                        rows[t.slot][:, c * RG:c * RG + D], start=(c == 0),
                                        stop=(c == t.chunks - 1))
                    last.then_inc(L.group_summed, 1)

            def step(w):
                L, B = layers[0], first_table
                cur, t1, t3, t5 = (w.back(k) for k in (0, 1, 3, 5))
                if cur:
                    words_of(cur, 0)
                if t3:
                    spread_s2(L, t3, 0)
                if t5:
                    turn_probs(L, t5, 0)
                if t1:
                    starts(t1)
                if cur:
                    words_of(cur, 1)
                if t1:
                    pack_edges(t1)
                if t3:
                    for k in range(1, len(t3.segments)):
                        spread_s2(L, t3, k)
                if t5:
                    sum_rows(L, t5)
                if w.s == 0:
                    make_table(B, PIECES)
                if w.s == 3:
                    mean(B)

            def step2(w):
                L = layers[1]
                t2, t3, t5 = w.back(2), w.back(3), w.back(5)
                if t5:
                    turn_probs(L, t5, 0)
                if t3:
                    for k in range(1, len(t3.segments)):
                        spread_s2(L, t3, k)
                if t2:
                    spread_s2(L, t2, 0)
                if t5:
                    sum_rows(L, t5)
                if w.s == 2:
                    pe.wait_ge(h_summed, 1)
                    T.matmul(sum_ps[:, 0:D], ones[:, :], h_sum[:, 0:D], start=True, stop=True
                             ).then_inc(h_mean, 1)
                    pe.wait_ge(h_total, 1)

            def chunk_of(sc, c):
                if c < HEAD:
                    return sc[:, c * P:(c + 1) * P]
                return sc[:, HEAD * P:N].rearrange("p (k t) -> p t k", t=TAIL)[:, c - HEAD, :]

            def dense_attend(L):
                with pe.Fori(0, NT) as i:
                    pe.wait_ge(L.probs, i + 1)
                    for q in range(NT // 4):
                        for k in range(4):
                            last = T.transpose(turned_ps[:, k * P:(k + 1) * P],
                                               chunk_of(dense_scores, 4 * q + k), identity[:, :])
                        last.then_inc(L.turned, 1)
                        pe.wait_ge(L.copied, i * (NT // 4) + (q + 1))
                        for k in range(4):
                            c = 4 * q + k
                            last = T.matmul(sum_ps[:, 0:D], probsT[0][:, k * P:(k + 1) * P],
                                            table3[:, c, 0:D], start=(c == 0), stop=(c == NT - 1))
                    last.then_inc(L.summed, 1)

            B = first_table
            pe.wait_ge(consts, 9)
            pe.wait_ge(w_in, 6 * 16)
            turn_weights(B)
            pe.wait_ge(dve_c, 1 + sum(len(units_of(t)) for t in range(HEAD)) + 1 + BITS)
            each_step(pe, NT, 5, step)
            pe.wait_ge(fault_made, 1)
            T.matmul(edges_ps[0:1, 256:257], fault[:, 2:3], fault[:, 3:4], start=True, stop=True
                     ).then_inc(fault_sum, 1)
            pe.wait_ge(flag_made, 1)
            dense = pe.value_load(flag[0:1, 0:1], min_val=0, max_val=1)
            with pe.If(dense < 1):
                each_step(pe, NT, 5, step2)
            with pe.If(dense > 0):
                for L, B in zip(dense_layers, dense_tables):
                    if L.n == 0:
                        pe.wait_ge(B.h, 1)
                        turn_weights(B)
                    make_table(B, 1)
                    mean(B)
                    pe.wait_ge(B.mean, 1)
                    dense_attend(L)


_INS = ["x", "adj", "L0_gnn_W", "L0_gnn_a", "L1_gnn_a"]


def kernel(**inputs):
    import numpy as np
    import concourse.bacc as bacc
    from concourse.bass_utils import run_bass_kernel_spmd

    nc = bacc.Bacc("TRN2", target_bir_lowering=False, num_devices=1)
    arrays = {f"in_{name}": np.ascontiguousarray(inputs[name]) for name in _INS}
    aps = [nc.dram_tensor(name, a.shape, mybir.dt.from_np(a.dtype), kind="ExternalInput").ap()
           for name, a in arrays.items()]
    out = nc.dram_tensor("out", arrays["in_x"].shape, F32, kind="ExternalOutput").ap()
    gat_kernel(nc, *aps, out)
    return run_bass_kernel_spmd(nc, [arrays], core_ids=[0]).results[0]["out"]
```
